# Optimizing a Trainium2 kernel written in Bass

```python
import numpy as np
import jax
import jax.numpy as jnp

def _softmax(x, axis=-1):
    return jax.nn.softmax(x, axis=axis)

def _gelu(x):
    return jax.nn.gelu(x, approximate=True)

def _silu(x):
    return jax.nn.silu(x)

def _sigmoid(x):
    return jax.nn.sigmoid(x)

def _layernorm(x, axis=-1, eps=1e-05):
    m = jnp.mean(x, axis=axis, keepdims=True)
    v = jnp.var(x, axis=axis, keepdims=True)
    return (x - m) / jnp.sqrt(v + eps)

def _scatter_add(tgt, idx, src, axis=0):
    return tgt.at[idx].add(src)

def _segment_sum(src, seg, n):
    return jax.ops.segment_sum(src, seg, n)
kernel_name = 'mk_macaron_d1_jaxref_r4_faade3'

def setup_inputs(seed: int=0):
    np.random.seed(seed)
    _w = jnp.asarray

    def _L0_attn_setup():
        import jax, jax.numpy as jnp
        import numpy as np
        B, S, H = (16, 128, 512)
        NH, NKV = (16, 4)
        HD = H // NH

        def _rope_tables(seq_len, dim, dtype):
            inv_freq = 1.0 / 10000.0 ** (jnp.arange(0, dim, 2, dtype=jnp.float32) / dim)
            t = jnp.arange(seq_len, dtype=jnp.float32)
            freqs = jnp.einsum('i,j->ij', t, inv_freq)
            emb = jnp.concatenate([freqs, freqs], axis=-1)
            cos = jnp.cos(emb)[None, None].astype(dtype)
            sin = jnp.sin(emb)[None, None].astype(dtype)
            return (cos, sin)

        def _rotate_half(x):
            x1, x2 = jnp.split(x, 2, axis=-1)
            return jnp.concatenate([-x2, x1], axis=-1)
        key = jax.random.key(seed)
        kx, kq, kk, kv, ko = jax.random.split(key, 5)
        x = jax.random.normal(kx, (B, S, H), dtype=jnp.float32)
        s = 0.02
        Wq = jax.random.normal(kq, (H, H), dtype=jnp.float32) * s
        Wk = jax.random.normal(kk, (NKV * HD, H), dtype=jnp.float32) * s
        Wv = jax.random.normal(kv, (NKV * HD, H), dtype=jnp.float32) * s
        Wo = jax.random.normal(ko, (H, H), dtype=jnp.float32) * s
        return {'x': x, 'Wq': Wq, 'Wk': Wk, 'Wv': Wv, 'Wo': Wo}
    _L0_attn_in = _L0_attn_setup()

    def _L0_ffn_setup():
        import jax, jax.numpy as jnp
        import numpy as np
        D = 512
        F = 352
        E = 8
        TOPK = 2
        N_SHARED = 2
        ROUTE_SCALE = 1.0

        def _swiglu(x, w1, w2, w3):
            return jax.nn.silu(x @ w1) * (x @ w3) @ w2
        key = jax.random.key(seed)
        ks = jax.random.split(key, 8)
        s = 0.02
        x = jax.random.normal(ks[0], (2, 256, D), dtype=jnp.float32)
        gate_w = jax.random.normal(ks[1], (D, E), dtype=jnp.float32) * s
        Fs = F * N_SHARED
        sw1 = jax.random.normal(ks[2], (D, Fs), dtype=jnp.float32) * s
        sw2 = jax.random.normal(ks[3], (Fs, D), dtype=jnp.float32) * s
        sw3 = jax.random.normal(ks[4], (D, Fs), dtype=jnp.float32) * s
        rw1 = jax.random.normal(ks[5], (E, D, F), dtype=jnp.float32) * s
        rw2 = jax.random.normal(ks[6], (E, F, D), dtype=jnp.float32) * s
        rw3 = jax.random.normal(ks[7], (E, D, F), dtype=jnp.float32) * s
        return {'x': x, 'gate_w': gate_w, 'sw1': sw1, 'sw2': sw2, 'sw3': sw3, 'rw1': rw1, 'rw2': rw2, 'rw3': rw3}
    _L0_ffn_in = _L0_ffn_setup()
    _d = {'L0_attn_x': _L0_attn_in['x'], 'L0_attn_Wq': _L0_attn_in['Wq'], 'L0_attn_Wk': _L0_attn_in['Wk'], 'L0_attn_Wv': _L0_attn_in['Wv'], 'L0_attn_Wo': _L0_attn_in['Wo'], 'L0_ffn_gate_w': _L0_ffn_in['gate_w'], 'L0_ffn_sw1': _L0_ffn_in['sw1'], 'L0_ffn_sw2': _L0_ffn_in['sw2'], 'L0_ffn_sw3': _L0_ffn_in['sw3'], 'L0_ffn_rw1': _L0_ffn_in['rw1'], 'L0_ffn_rw2': _L0_ffn_in['rw2'], 'L0_ffn_rw3': _L0_ffn_in['rw3']}
    _x0 = _d['L0_attn_x']
    _d['L0_attn_x'] = jax.random.normal(jax.random.fold_in(jax.random.key(seed), 1), (2, 1024, 512), dtype=_x0.dtype)
    del _x0
    return _d

def reference(L0_attn_x, L0_attn_Wq, L0_attn_Wk, L0_attn_Wv, L0_attn_Wo, L0_ffn_gate_w, L0_ffn_sw1, L0_ffn_sw2, L0_ffn_sw3, L0_ffn_rw1, L0_ffn_rw2, L0_ffn_rw3):

    def _L0_attn_ref(x, Wq, Wk, Wv, Wo):
        import jax, jax.numpy as jnp
        import numpy as np
        B, S, H = (16, 128, 512)
        NH, NKV = (16, 4)
        HD = H // NH

        def _rope_tables(seq_len, dim, dtype):
            inv_freq = 1.0 / 10000.0 ** (jnp.arange(0, dim, 2, dtype=jnp.float32) / dim)
            t = jnp.arange(seq_len, dtype=jnp.float32)
            freqs = jnp.einsum('i,j->ij', t, inv_freq)
            emb = jnp.concatenate([freqs, freqs], axis=-1)
            cos = jnp.cos(emb)[None, None].astype(dtype)
            sin = jnp.sin(emb)[None, None].astype(dtype)
            return (cos, sin)

        def _rotate_half(x):
            x1, x2 = jnp.split(x, 2, axis=-1)
            return jnp.concatenate([-x2, x1], axis=-1)
        b, s, _ = x.shape
        scaling = HD ** (-0.5)
        q = jnp.einsum('bsh,oh->bso', x, Wq).reshape(b, s, NH, HD).transpose(0, 2, 1, 3)
        k = jnp.einsum('bsh,oh->bso', x, Wk).reshape(b, s, NKV, HD).transpose(0, 2, 1, 3)
        v = jnp.einsum('bsh,oh->bso', x, Wv).reshape(b, s, NKV, HD).transpose(0, 2, 1, 3)
        cos, sin = _rope_tables(s, HD, x.dtype)
        q = q * cos + _rotate_half(q) * sin
        k = k * cos + _rotate_half(k) * sin
        rep = NH // NKV
        k = jnp.repeat(k, rep, axis=1)
        v = jnp.repeat(v, rep, axis=1)
        scores = jnp.einsum('bhqd,bhkd->bhqk', q, k) * scaling
        attn = jax.nn.softmax(scores, axis=-1)
        out = jnp.einsum('bhqk,bhkd->bhqd', attn, v)
        out = out.transpose(0, 2, 1, 3).reshape(b, s, H)
        return jnp.einsum('bsh,oh->bso', out, Wo)

    def _L0_ffn_ref(x, gate_w, sw1, sw2, sw3, rw1, rw2, rw3):
        import jax, jax.numpy as jnp
        import numpy as np
        D = 512
        F = 352
        E = 8
        TOPK = 2
        N_SHARED = 2
        ROUTE_SCALE = 1.0

        def _swiglu(x, w1, w2, w3):
            return jax.nn.silu(x @ w1) * (x @ w3) @ w2
        B, T, _ = x.shape
        xf = x.reshape(-1, D)
        N = xf.shape[0]
        y = _swiglu(xf, sw1, sw2, sw3)
        scores = jax.nn.softmax(xf @ gate_w, axis=-1)
        weights, indices = jax.lax.top_k(scores, TOPK)
        weights = weights * ROUTE_SCALE
        cw = jnp.zeros((N, E), dtype=xf.dtype).at[jnp.arange(N)[:, None], indices].add(weights)
        for e in range(E):
            h = _swiglu(xf, rw1[e], rw2[e], rw3[e])
            y = y + cw[:, e:e + 1] * h
        return y.reshape(B, T, D)
    x = L0_attn_x
    x = x + 0.5 * _L0_ffn_ref(_layernorm(x, axis=-1), L0_ffn_gate_w, L0_ffn_sw1, L0_ffn_sw2, L0_ffn_sw3, L0_ffn_rw1, L0_ffn_rw2, L0_ffn_rw3)
    x = x + _L0_attn_ref(_layernorm(x, axis=-1), L0_attn_Wq, L0_attn_Wk, L0_attn_Wv, L0_attn_Wo)
    x = x + 0.5 * _L0_ffn_ref(_layernorm(x, axis=-1), L0_ffn_gate_w, L0_ffn_sw1, L0_ffn_sw2, L0_ffn_sw3, L0_ffn_rw1, L0_ffn_rw2, L0_ffn_rw3)
    return x

_drawn_inputs = setup_inputs


def setup_inputs(seed=0):
    import zlib

    import numpy as np

    out = dict(_drawn_inputs(seed))
    spreads = {}
    factors = {'L0_attn_Wq': 8.0,
     'L0_attn_Wk': 8.0,
     'L0_attn_Wv': 8.0,
     'L0_attn_Wo': 8.0,
     'L0_ffn_gate_w': 5.597,
     'L0_ffn_rw1': 4.945,
     'L0_ffn_rw2': 4.833,
     'L0_ffn_rw3': 4.848}
    for name, (base, spread) in spreads.items():
        noise = np.random.default_rng([zlib.crc32(name.encode()), seed]).standard_normal(out[name].shape)
        drawn = base * np.exp(spread * noise) if base else spread * noise
        out[name] = jnp.asarray(drawn.astype(out[name].dtype))
    for name, factor in factors.items():
        out[name] = (out[name] * factor).astype(out[name].dtype)
    return out
```

```python
import numpy as np

import concourse.bass as bass
from concourse import mybir

P = 128
B, S, D = 2, 1024, 512
TOK = B * S
NT = TOK // P
DC = D // P
GRP = 512
NG = TOK // GRP
TPG = GRP // P
F, E, N_SHARED = 352, 8, 2
FS = F * N_SHARED
HID = FS + E * F
NCH = -(-HID // P)
SUPER = 4
NSUP = NCH // SUPER
SHARED_ONLY = FS // P
WCOL = 2 * D + D
NH, NKV = 16, 4
HD = D // NH
REP = NH // NKV
QT = S // P
SCALE = float(HD) ** -0.5
EPS = 1e-5
STK = 3 * HD
ROWS = STK + 2

F32 = mybir.dt.float32
F32R = mybir.dt.float32r
BF16 = mybir.dt.bfloat16
ALU = mybir.AluOpType
ACT = mybir.ActivationFunctionType
AX = mybir.AxisListType


def ACTIVATION(e, *args, **kw):
    return e.activation(*args, **kw)


def BN_AGGR(e, *args, **kw):
    return e.bn_aggr(*args, **kw)


def BN_STATS(e, *args, **kw):
    return e.bn_stats(*args, **kw)


def MATCH_REPLACE(e, *args, **kw):
    return e.match_replace(*args, **kw)


def MATMUL(e, *args, **kw):
    return e.matmul(*args, **kw)


def MAX(e, *args, **kw):
    return e.max(*args, **kw)


def MEMSET(e, *args, **kw):
    return e.memset(*args, **kw)


def RECIPROCAL(e, *args, **kw):
    return e.reciprocal(*args, **kw)


def SCALAR_TENSOR_TENSOR(e, *args, **kw):
    return e.scalar_tensor_tensor(*args, **kw)


def TENSOR_COPY(e, *args, **kw):
    return e.tensor_copy(*args, **kw)


def TENSOR_REDUCE(e, *args, **kw):
    return e.tensor_reduce(*args, **kw)


def TENSOR_SCALAR(e, *args, **kw):
    return e.tensor_scalar(*args, **kw)


def TENSOR_TENSOR(e, *args, **kw):
    return e.tensor_tensor(*args, **kw)


def TRANSPOSE(e, *args, **kw):
    return e.transpose(*args, **kw)


class Queue:

    def __init__(self, nc, ctx, name):
        self.sem = ctx.enter_context(nc.semaphore(f"{name}_done"))
        self.todo, self.count, self.seen = [], 0, {}

    def do(self, instruction, *args, tick=True, **kw):
        if tick:
            self.count += 1
            self.todo.append(lambda e: instruction(e, *args, **kw).then_inc(self.sem, 1))
        else:
            self.todo.append(lambda e: instruction(e, *args, **kw))
        return (self.sem, self.count) if tick else None

    def wait(self, *events):
        for event in events:
            if event is None:
                continue
            sem, value = event
            if self.seen.get(id(sem), 0) < value:
                self.seen[id(sem)] = value
                self.todo.append(lambda e, s=sem, v=value: e.wait_ge(s, v))

    def last(self):
        return (self.sem, self.count)

    def emit(self, engine):
        for step in self.todo:
            step(engine)


class Landing:

    def __init__(self, nc, ctx, name):
        self.sem, self.count = ctx.enter_context(nc.semaphore(name)), 0

    def start(self, queue, out, in_):
        self.count += 16
        queue.todo.append(lambda e: e.dma_start(out, in_).then_inc(self.sem, 16))
        return (self.sem, self.count)


def macaron(nc, ctx, x, ffn_w, gate_w, wqkv, wo, sel, rope, ident, out):
    base = -(-nc.sbuf_base // 64) * 64
    used = {}

    def place(name, shape, dt, at):
        size = int(np.prod(shape[1:])) * (2 if dt == BF16 else 4)
        at = -(-at // 32) * 32
        used[name] = (at, at + size)
        assert at + size <= nc.sbuf_usable_end, (name, at + size - nc.sbuf_usable_end)
        return nc.alloc_sbuf_tensor_at(name, list(shape), dt, offset=at), at + size

    at = base
    X, at = place("X", (P, NT, D), F32, at)
    identf, at = place("identf", (P, P), F32, at)
    identb, at = place("identb", (P, P), BF16, at)
    mv, at = place("mv", (P, NT, 2), F32, at)
    stats, at = place("stats", (P, 2, 6), F32, at)
    rstd, at = place("rstd", (P, NT), F32, at)
    ve, at = place("ve", (P, NT), F32, at)
    nwt, at = place("nwt", (P, NT), F32, at)
    xT0 = at
    xTh, at = place("xTh", (P, DC, TOK), F32R, at)
    xTl, at = place("xTl", (P, DC, TOK), F32R, at)
    ph0 = at
    xn, at = place("xn", (P, 2, D), F32, at)
    ph1 = at

    RING = 5
    Wh, at = place("Wh", (P, RING, WCOL), F32R, at)
    Wl, at = place("Wl", (P, RING, WCOL), F32R, at)
    raw, at = place("raw", (P, 1, WCOL), F32, at)
    silu, at = place("silu", (P, 2, GRP), F32, at)
    hid, at = place("hid", (P, 2, GRP), F32, at)
    hidh, at = place("hidh", (P, 2, GRP), F32R, at)
    hidl, at = place("hidl", (P, 2, GRP), F32R, at)
    selS, at = place("selS", (P, NCH * P), BF16, at)
    cwT, at = place("cwT", (P, TOK), BF16, at)
    gf, at = place("gf", (P, DC, E), F32, at)
    gh, at = place("gh", (P, DC, E), F32R, at)
    gl, at = place("gl", (P, DC, E), F32R, at)
    rt = used["Wl"][1] - WCOL * 4
    l16, rt = place("l16", (P, NT, 2 * E), F32, rt)
    r16, rt = place("r16", (P, NT, 2 * E), F32, rt)
    m8, rt = place("m8", (P, NT, 8), F32, rt)
    rmx, rt = place("rmx", (P, NT), F32, rt)
    rsm, rt = place("rsm", (P, NT), F32, rt)
    cw, rt = place("cw", (P, NT, E), F32, rt)
    assert rt <= used["Wl"][1]
    cwb_at = used["Wh"][1] - WCOL * 4
    cwb, _ = place("cwb", (P, NT, P), BF16, cwb_at)

    at = ph1
    qtok, at = place("qtok", (P, NT, D), F32, at)
    KS, at = place("KS", (P, B, NKV, S), F32R, at)
    V, at = place("V", (P, NT, NKV, HD + 1), F32, at)
    ropeS, at = place("ropeS", (P, QT, 2, HD), F32, at)
    kst, at = place("kst", (P, NKV, STK), F32, at)
    qkr, at = place("qkr", (P, NH + NKV, HD), F32, at)
    qka, at = place("qka", (P, NH + NKV, HD), F32, at)
    wqkv_end = at
    Wqh, at = place("Wqh", (P, DC, D + 2 * NKV * HD), F32R, at)
    OT, _ = place("OT", (P, GRP), F32, wqkv_end)
    TS, _ = place("TS", (P, 2, REP, STK), F32, wqkv_end + 2048)
    Wql, at2 = place("Wql", (P, DC, D + 2 * NKV * HD), F32R, at)
    wraw, _ = place("wraw", (P, DC, D + 2 * NKV * HD), F32, used["qtok"][0])
    at = xT0
    QRING = 3 * REP
    QS, at = place("QS", (P, QRING, S), F32R, at)
    PT, at = place("PT", (P, 3, 2 * GRP), F32, at)
    nm, at = place("nm", (P, QRING, 2 * QT), F32, at)
    nmf, at = place("nmf", (P, QRING, QT), F32, at)
    MT, at = place("MT", (2 * QT, 2, P), F32, at)
    rL, at = place("rL", (P, 2, TPG), F32, at)
    assert at <= ph0
    Woh, at = place("Woh", (P, DC, D), F32R, used["KS"][0])
    Wol, at = place("Wol", (P, DC, D), F32R, at)
    woraw, _ = place("woraw", (P, DC, D), F32, at)

    PS = ctx.enter_context(nc.psum_tensor("PS", [P, 8, GRP], F32))

    pe, act, dve, pool, sp = (Queue(nc, ctx, n) for n in ("pe", "act", "dve", "pool", "sp"))
    load = [Landing(nc, ctx, f"load{i}") for i in range(12)]
    in_x = [Landing(nc, ctx, f"in_x{g}") for g in range(NG)]
    in_w = Landing(nc, ctx, "in_w")
    in_m = [Landing(nc, ctx, f"in_m{i}") for i in range(QRING)]
    out_x = [Landing(nc, ctx, f"out_x{g}") for g in range(NG)]
    bank_free = [None] * 8

    def phase_end():
        ends = [q.last() for q in (pe, act, dve, pool)]
        for q in (pe, act, dve, pool, sp):
            q.wait(*ends)

    def mm3(dst, lh, ll, rh, rl, first, last):
        pe.do(MATMUL, dst, lh, rh, start=first, stop=False, tick=False)
        pe.do(MATMUL, dst, lh, rl, start=False, stop=False, tick=False)
        return pe.do(MATMUL, dst, ll, rh, start=False, stop=last, tick=last)

    x_in = []
    id_in = load[0].start(sp, identf[:], ident)
    for g in range(NG):
        x_in.append(in_x[g].start(sp, X[:, g * TPG:(g + 1) * TPG, :],
                                  x[g * GRP:(g + 1) * GRP, :].rearrange("(t p) d -> p t d", p=P)))
    dve.wait(id_in)
    consts = dve.do(TENSOR_COPY, identb[:], identf[:])

    X_ready = list(x_in)

    def to_columns(t, src, src_ready, bank, wait_dst):
        pe.wait(src_ready, bank_free[bank], id_in)
        for c in range(DC):
            turned = pe.do(TRANSPOSE, PS[:, bank, c * P:(c + 1) * P],
                                                      src[:, c * P:(c + 1) * P], identf[:], tick=(c == DC - 1))
        tile = PS[:, bank, :].rearrange("p (c n) -> p c n", c=DC)
        act.wait(turned, *wait_dst)
        hi = act.do(ACTIVATION, xTh[:, :, t * P:(t + 1) * P], tile, ACT.Copy)
        dve.wait(turned, hi)
        lo = dve.do(TENSOR_TENSOR, xTl[:, :, t * P:(t + 1) * P], tile,
                                              xTh[:, :, t * P:(t + 1) * P], ALU.subtract)
        bank_free[bank] = lo
        return turned, lo

    xn_free = [None, None]

    def layer_norm(wait_dst):
        ready = []
        for g in range(NG):
            ts = slice(g * TPG, (g + 1) * TPG)
            dve.wait(X_ready[g])
            for t in range(g * TPG, (g + 1) * TPG):
                st = dve.do(BN_STATS, stats[:, t % 2, :], X[:, t, :])
                dve.wait(st)
                done = dve.do(BN_AGGR, mv[:, t, :], stats[:, t % 2, :])
            dve.wait(done)
            v = dve.do(TENSOR_SCALAR, ve[:, ts], mv[:, ts, 1], EPS, None, ALU.add)
            act.wait(v)
            sq = act.do(ACTIVATION, rstd[:, ts], ve[:, ts], ACT.Sqrt)
            dve.wait(sq)
            r = dve.do(RECIPROCAL, rstd[:, ts], rstd[:, ts])
            for a, b in ((rstd, rstd), (nwt, ve)):
                dve.wait(r)
                r = dve.do(TENSOR_TENSOR, nwt[:, ts], a[:, ts], b[:, ts], ALU.mult)
            dve.wait(r)
            r = dve.do(TENSOR_SCALAR, nwt[:, ts], nwt[:, ts], -0.5, 1.5, ALU.mult, ALU.add)
            dve.wait(r)
            r = dve.do(TENSOR_TENSOR, rstd[:, ts], rstd[:, ts], nwt[:, ts], ALU.mult)
            dve.wait(r)
            for t in range(g * TPG, (g + 1) * TPG):
                dve.wait(xn_free[t % 2])
                n = dve.do(TENSOR_SCALAR, xn[:, t % 2, :], X[:, t, :], mv[:, t, 0:1],
                                                          rstd[:, t:t + 1], ALU.subtract, ALU.mult)
                xn_free[t % 2], lo = to_columns(t, xn[:, t % 2, :], n, 4 + t % 4, wait_dst)
            ready.append(lo)
        return ready

    def ffn(number):
        w_ready, w_free = [None] * NCH, [None] * RING
        raw_free = [None]
        cwb_done = [None]

        def weights(k):
            sp.wait(raw_free[0])
            got = load[1].start(sp, raw[:, 0, :], ffn_w[k])
            s = k % RING
            pool.wait(got, w_free[s])
            hi = pool.do(TENSOR_COPY, Wh[:, s, :], raw[:, 0, :])
            pool.wait(hi)
            raw_free[0] = w_ready[k] = pool.do(TENSOR_TENSOR, Wl[:, s, :], raw[:, 0, :], Wh[:, s, :], ALU.subtract)

        got_gate = load[3].start(sp, gf[:], gate_w)
        pool.wait(got_gate)
        g1 = pool.do(TENSOR_COPY, gh[:], gf[:])
        pool.wait(g1)
        gate_ready = pool.do(TENSOR_TENSOR, gl[:], gf[:], gh[:], ALU.subtract)
        got_sel = load[2].start(sp, selS[:], sel)
        z1 = pool.do(MEMSET, l16[:], -1.0)
        z2 = pool.do(MEMSET, cwb[:], 0.0)
        pool.wait(z2)
        z3 = pool.do(MEMSET, cwb[:, :, 3 * E:3 * E + 1], 1.0)
        for k in range(RING - 1):
            weights(k)

        x_ready = layer_norm([])

        bank = 3
        pe.wait(gate_ready, x_ready[-1], bank_free[bank])
        for t in range(NT):
            dst = PS[:, bank, t * E:(t + 1) * E]
            ts = slice(t * P, (t + 1) * P)
            for c in range(DC):
                logits = mm3(dst, xTh[:, c, ts], xTl[:, c, ts], gh[:, c, :], gl[:, c, :], c == 0, c == DC - 1)
        lg = PS[:, bank, 0:NT * E].rearrange("p (t e) -> p t e", e=E)
        dve.wait(logits)
        r = dve.do(TENSOR_REDUCE, rmx[:], lg, AX.X, ALU.max)
        dve.wait(r, z1)
        r = dve.do(TENSOR_TENSOR, l16[:, :, 0:E], lg, rmx[:].unsqueeze(2).broadcast_to([P, NT, E]),
                                             ALU.subtract)
        bank_free[bank] = r
        act.wait(r)
        r = act.do(ACTIVATION, l16[:, :, 0:E], l16[:, :, 0:E], ACT.Exp)
        dve.wait(r)
        r = dve.do(TENSOR_REDUCE, rsm[:], l16[:, :, 0:E], AX.X, ALU.add)
        dve.wait(r)
        dve.do(RECIPROCAL, rsm[:], rsm[:])
        for t in range(NT):
            r = dve.do(MAX, m8[:, t, :], l16[:, t, :])
        dve.wait(r)
        r = dve.do(MEMSET, m8[:, :, 2:8], -1.0)
        dve.wait(r)
        for t in range(NT):
            r = dve.do(MATCH_REPLACE, r16[:, t, :], m8[:, t, :], l16[:, t, :], 0.0)
        dve.wait(r)
        r = dve.do(TENSOR_TENSOR, cw[:], l16[:, :, 0:E], r16[:, :, 0:E], ALU.subtract)
        dve.wait(r)
        r = dve.do(TENSOR_TENSOR, cw[:], cw[:], rsm[:].unsqueeze(2).broadcast_to([P, NT, E]), ALU.mult)
        dve.wait(z3)
        for part in range(3):
            dve.wait(r)
            dst = cwb[:, :, part * E:(part + 1) * E]
            r = dve.do(TENSOR_COPY, dst, cw[:])
            if part < 2:
                dve.wait(r)
                r = dve.do(TENSOR_TENSOR, cw[:], cw[:], dst, ALU.subtract)
        HB = NT // 2
        for half in range(2):
            bk = 6 + half
            turned_to = PS[:, bk, :].bitcast(BF16).rearrange("p (t n) -> p t n", n=P)
            pe.wait(r, consts, bank_free[bk])
            for i in range(HB):
                tr = pe.do(TRANSPOSE, turned_to[:, i, :], cwb[:, half * HB + i, :], identb[:],
                           tick=(i == HB - 1))
            dve.wait(tr)
            cw_ready = dve.do(TENSOR_COPY, 
                cwT[:, half * HB * P:(half + 1) * HB * P], PS[:, bk, :].bitcast(BF16))
            bank_free[bk] = cw_ready
        w_free[(RING - 1) % RING] = cw_ready
        weights(RING - 1)

        bufs = dict(silu=[None] * 2, hid=[None] * 2)
        pending = []
        Y_free = [bank_free[j] for j in range(4)]
        out_ready = [None] * NG
        step = [0]

        def second(item):
            k, c, g, s, i, ready = item
            pe.wait(ready)
            for j in range(TPG):
                if c == 0:
                    pe.wait(Y_free[j])
                js = slice(j * P, (j + 1) * P)
                hh, hl = hidh[:, i, js], hidl[:, i, js]
                w2h, w2l = Wh[:, s, 2 * D:], Wl[:, s, 2 * D:]
                dst = PS[:, j, :]
                first, last = c == 0, c == SUPER - 1
                pe.do(MATMUL, dst, hh, w2h, start=first, stop=False, tick=False)
                pe.do(MATMUL, dst, hh, w2l, start=False, stop=False, tick=False)
                done = pe.do(MATMUL, dst, hl, w2h, start=False, stop=last)
                if last:
                    dve.wait(done)
                    t = g * TPG + j
                    Y_free[j] = out_ready[g] = dve.do(SCALAR_TENSOR_TENSOR, 
                        X[:, t, :], dst, 0.5, X[:, t, :], ALU.mult, ALU.add)
            bufs["hid"][i] = done
            if g == NG - 1:
                w_free[s] = done
                if k + RING < NCH:
                    weights(k + RING)

        for sup in range(NSUP):
            for g in range(NG):
                gs = slice(g * GRP, (g + 1) * GRP)
                for c in range(SUPER):
                    k = sup * SUPER + c
                    s, i = k % RING, step[0] % 2
                    bank_a, bank_b, bank_m = (4, 7)[i], 5, 6
                    step[0] += 1
                    pe.wait(w_ready[k], x_ready[g])
                    for bank, col in ((bank_a, 0), (bank_b, D)):
                        pe.wait(bank_free[bank])
                        for d in range(DC):
                            ws = slice(col + d * P, col + (d + 1) * P)
                            done = mm3(PS[:, bank, :], Wh[:, s, ws], Wl[:, s, ws], xTh[:, d, gs], xTl[:, d, gs],
                                       d == 0, d == DC - 1)
                        if bank == bank_a:
                            a_done = done
                    b_done = done
                    routed = k >= SHARED_ONLY
                    if routed:
                        pe.wait(cw_ready, got_sel, bank_free[bank_m])
                        m_done = pe.do(MATMUL, PS[:, bank_m, :], selS[:, k * P:(k + 1) * P],
                                                                      cwT[:, gs], start=True, stop=True)
                    act.wait(a_done, bufs["silu"][i])
                    sl = act.do(ACTIVATION, silu[:, i, :], PS[:, bank_a, :], ACT.Silu)
                    bank_free[bank_a] = sl
                    dve.wait(sl, b_done, bufs["hid"][i])
                    h = dve.do(TENSOR_TENSOR, hid[:, i, :], silu[:, i, :], PS[:, bank_b, :], ALU.mult)
                    bank_free[bank_b] = bufs["silu"][i] = h
                    if routed:
                        dve.wait(h, m_done)
                        h = dve.do(TENSOR_TENSOR, hid[:, i, :], hid[:, i, :], PS[:, bank_m, :], ALU.mult)
                        bank_free[bank_m] = h
                    dve.wait(h)
                    hh = dve.do(TENSOR_COPY, hidh[:, i, :], hid[:, i, :])
                    dve.wait(hh)
                    hl = dve.do(TENSOR_TENSOR, hidl[:, i, :], hid[:, i, :], hidh[:, i, :], ALU.subtract)
                    pending.append((k, c, g, s, i, hl))
                    if len(pending) > 1:
                        second(pending.pop(0))
        second(pending.pop(0))
        for j in range(4):
            bank_free[j] = Y_free[j]
        for g in range(NG):
            X_ready[g] = out_ready[g]
        if number == 1:
            for g in range(NG):
                sp.wait(out_ready[g])
                out_x[g].start(sp, out[g * GRP:(g + 1) * GRP, :].rearrange("(t p) d -> p t d", p=P),
                               X[:, g * TPG:(g + 1) * TPG, :])

    def attention():
        QKV = D + 2 * NKV * HD
        got = load[4].start(sp, wraw[:], wqkv)
        got_rope = load[5].start(sp, ropeS[:], rope)
        pool.wait(got)
        hi = pool.do(TENSOR_COPY, Wqh[:], wraw[:])
        pool.wait(hi)
        w_ready = pool.do(TENSOR_TENSOR, Wql[:], wraw[:], Wqh[:], ALU.subtract)
        vones = pool.do(MEMSET, V[:, :, :, HD:HD + 1], 1.0)
        pool.wait(vones)
        ones = pool.do(MEMSET, KS[STK:ROWS, :, :, :].bitcast(F32), 1.0)

        h_ready = layer_norm([])

        kst_free = [None]
        for t in range(NT):
            bq = (t % 2) * 2
            ts = slice(t * P, (t + 1) * P)
            pe.wait(w_ready, h_ready[t // TPG], bank_free[bq], bank_free[bq + 1])
            for c in range(DC):
                mm3(PS[:, bq, :], xTh[:, c, ts], xTl[:, c, ts], Wqh[:, c, 0:D], Wql[:, c, 0:D], c == 0, c == DC - 1)
            for c in range(DC):
                done = mm3(PS[:, bq + 1, 0:QKV - D], xTh[:, c, ts], xTl[:, c, ts], Wqh[:, c, D:], Wql[:, c, D:],
                           c == 0, c == DC - 1)
            qk = PS[:, bq:bq + 2, :].rearrange("p b n -> p (b n)")[:, 0:D + NKV * HD].rearrange("p (h d) -> p h d", d=HD)
            half = HD // 2
            cos = ropeS[:, t % QT, 0:1, :].broadcast_to([P, NH + NKV, HD])
            sin = ropeS[:, t % QT, 1:2, :].broadcast_to([P, NH + NKV, HD])
            dve.wait(done, got_rope, w_ready)
            dve.do(TENSOR_TENSOR, qka[:], qk, cos, ALU.mult)
            dve.do(TENSOR_TENSOR, qkr[:, :, 0:half], qk[:, :, half:], sin[:, :, 0:half], ALU.mult)
            r = dve.do(TENSOR_TENSOR, qkr[:, :, half:], qk[:, :, 0:half], sin[:, :, half:], ALU.mult)
            act.wait(r, ones)
            v = act.do(ACTIVATION, 
                V[:, t, :, 0:HD], PS[:, bq + 1, NKV * HD:2 * NKV * HD].rearrange("p (h d) -> p h d", d=HD), ACT.Copy)
            dve.wait(r)
            r = dve.do(TENSOR_TENSOR, 
                qtok[:, t, :].rearrange("p (h d) -> p h d", d=HD), qka[:, 0:NH, :], qkr[:, 0:NH, :], ALU.add)
            bank_free[bq] = bank_free[bq + 1] = v
            r = dve.do(TENSOR_TENSOR, qka[:, NH:, :], qka[:, NH:, :], qkr[:, NH:, :], ALU.add)
            dve.wait(r, kst_free[0])
            r = dve.do(TENSOR_COPY, kst[:, :, 0:HD].bitcast(F32R), qka[:, NH:, :])
            dve.wait(r)
            dve.do(TENSOR_COPY, kst[:, :, HD:2 * HD], kst[:, :, 0:HD])
            r = dve.do(TENSOR_TENSOR, kst[:, :, 2 * HD:].bitcast(F32R), qka[:, NH:, :], kst[:, :, 0:HD], ALU.subtract)
            bk = 4 + t % 2
            pe.wait(r, bank_free[bk])
            for h in range(NKV):
                tr = pe.do(TRANSPOSE, PS[0:STK, bk, h * P:(h + 1) * P], kst[:, h, :], identf[:],
                           tick=(h == NKV - 1))
            kst_free[0] = tr
            act.wait(tr)
            bank_free[bk] = act.do(ACTIVATION, 
                KS[0:STK, t // QT, :, (t % QT) * P:(t % QT + 1) * P],
                PS[0:STK, bk, :].rearrange("p (h n) -> p h n", n=P), ACT.Copy)
        phase_end()

        groups = [(b, g) for b in range(B) for g in range(NKV)]
        ts_free = [None, None]
        MISC, OB = 7, 6
        q_ready = {}
        m_ready = {}
        pair_free = [[bank_free[2 * i], bank_free[2 * i + 1]] for i in range(3)]
        turn = [0]

        def stack_queries(n, t):
            b, g = groups[n]
            tile, i = b * QT + t, t % 2
            src = qtok[:, tile, g * REP * HD:(g + 1) * REP * HD].rearrange("p (h d) -> p h d", d=HD)
            dve.wait(ts_free[i])
            r = dve.do(TENSOR_COPY, TS[:, i, :, 0:HD].bitcast(F32R), src)
            dve.wait(r)
            dve.do(TENSOR_COPY, TS[:, i, :, 2 * HD:], TS[:, i, :, 0:HD])
            r = dve.do(TENSOR_TENSOR, TS[:, i, :, HD:2 * HD].bitcast(F32R), src, TS[:, i, :, 0:HD], ALU.subtract)
            pe.wait(r, bank_free[MISC])
            for h in range(REP):
                tr = pe.do(TRANSPOSE, PS[0:STK, MISC, h * P:(h + 1) * P], TS[:, i, h, :], identf[:],
                           tick=(h == REP - 1))
            ts_free[i] = tr
            s0 = (n % 3) * REP
            act.wait(tr)
            q_ready[n] = bank_free[MISC] = act.do(ACTIVATION, 
                QS[0:STK, s0:s0 + REP, t * P:(t + 1) * P], PS[0:STK, MISC, :].rearrange("p (h n) -> p h n", n=P), ACT.Copy)

        def take_pair():
            i = turn[0] % 3
            turn[0] += 1
            pe.wait(*pair_free[i])
            return i

        def row_max(n, h, t):
            b, g = groups[n]
            s = (n % 3) * REP + h
            i = take_pair()
            pe.wait(q_ready[n])
            for half in range(2):
                done = pe.do(MATMUL, PS[:, 2 * i + half, :], QS[0:STK, s, t * P:(t + 1) * P],
                                                           KS[0:STK, b, g, half * GRP:(half + 1) * GRP],
                                                           start=True, stop=True, tick=(half == 1))
            dve.wait(done)
            r = dve.do(TENSOR_REDUCE, nmf[:, s, t:t + 1], PS[:, 2 * i:2 * i + 2, :].rearrange("p b n -> p (b n)"),
                                                 AX.X, ALU.max, negate=True)
            pair_free[i] = [r]
            if t == QT - 1:
                dve.wait(r)
                r = dve.do(TENSOR_COPY, nm[:, s, 0:QT].bitcast(F32R), nmf[:, s, :])
                dve.wait(r)
                r = dve.do(TENSOR_TENSOR, nm[:, s, QT:].bitcast(F32R), nmf[:, s, :], nm[:, s, 0:QT], ALU.subtract)
                pe.wait(r, bank_free[MISC])
                tr = pe.do(TRANSPOSE, PS[0:2 * QT, MISC, 0:P], nm[:, s, :], identf[:])
                j = h % 2
                act.wait(tr, mt_free[j])
                bank_free[MISC] = r = act.do(ACTIVATION, MT[:, j, :], PS[0:2 * QT, MISC, 0:P], ACT.Copy)
                sp.wait(r)
                for part in range(2):
                    m_ready[(n, h)] = mt_free[j] = in_m[s].start(
                        sp, QS[STK + part:STK + part + 1, s, :].bitcast(F32).rearrange("p (t n) -> p t n", n=P),
                        MT[part * QT:(part + 1) * QT, j, :])

        mt_free = [None, None]
        pt_free = [None] * 3
        pending = []
        ot_free = [None]
        rl_free = [None, None]
        segs = [0]

        def attend_first(n, h, half, pair, u):
            b, g = groups[n]
            s = (n % 3) * REP + h
            i = take_pair()
            pe.wait(m_ready[(n, h)])
            for j in range(2):
                kt = 2 * pair + j
                done = pe.do(MATMUL, PS[:, 2 * i + j, :], KS[0:ROWS, b, g, kt * P:(kt + 1) * P],
                                                            QS[0:ROWS, s, half * GRP:(half + 1) * GRP],
                                                            start=True, stop=True, tick=(j == 1))
            k = u % 3
            act.wait(done, pt_free[k])
            r = act.do(ACTIVATION, PT[:, k, :], PS[:, 2 * i:2 * i + 2, :].rearrange("p b n -> p (b n)"),
                                              ACT.Exp, scale=SCALE)
            pair_free[i] = [r]
            pending.append((n, h, half, pair, k, r))

        def attend_second(item):
            n, h, half, pair, k, ready = item
            b, g = groups[n]
            pe.wait(ready)
            if pair == 0:
                pe.wait(bank_free[OB])
            for j in range(2):
                kt = 2 * pair + j
                done = pe.do(MATMUL, PS[0:HD + 1, OB, :], V[:, b * QT + kt, g, :],
                                                            PT[:, k, j * GRP:(j + 1) * GRP],
                                                            start=(kt == 0), stop=(kt == QT - 1), tick=(j == 1))
            pt_free[k] = done
            if pair == QT // 2 - 1:
                act.wait(done, ot_free[0])
                bank_free[OB] = r = act.do(ACTIVATION, OT[0:HD + 1, :], PS[0:HD + 1, OB, :], ACT.Copy)
                finish.append((n, h, half, r))

        finish = []

        def store_head(item):
            n, h, half, r = item
            b, g = groups[n]
            pe.wait(r, bank_free[MISC])
            W = HD + 1
            for j in range(TPG):
                tr = pe.do(TRANSPOSE, PS[:, MISC, j * W:(j + 1) * W], OT[0:W, j * P:(j + 1) * P],
                                                      identf[0:W, 0:W], tick=(j == TPG - 1))
            ot_free[0] = tr
            o = PS[:, MISC, 0:TPG * W].rearrange("p (j w) -> p j w", w=W)
            q = segs[0] % 2
            segs[0] += 1
            dve.wait(tr)
            r = dve.do(RECIPROCAL, rL[:, q, :], o[:, :, HD])
            dve.wait(r)
            t0 = b * QT + half * TPG
            c0 = (g * REP + h) * HD
            bank_free[MISC] = dve.do(TENSOR_TENSOR, 
                qtok[:, t0:t0 + TPG, c0:c0 + HD], o[:, :, 0:HD],
                rL[:, q, :].unsqueeze(2).broadcast_to([P, TPG, HD]), ALU.mult)

        for n in range(2):
            for t in range(QT):
                stack_queries(n, t)
        for h in range(REP):
            for t in range(QT):
                row_max(0, h, t)
        for n in range(len(groups)):
            u = 0
            for h in range(REP):
                for half in range(2):
                    for pair in range(QT // 2):
                        attend_first(n, h, half, pair, u)
                        if n + 1 < len(groups):
                            row_max(n + 1, u // QT, u % QT)
                        if len(pending) > 1:
                            attend_second(pending.pop(0))
                        if len(finish) and pair == 2:
                            store_head(finish.pop(0))
                        if n + 2 < len(groups) and u % 4 == 3:
                            stack_queries(n + 2, u // 4)
                        u += 1
        attend_second(pending.pop(0))
        while finish:
            store_head(finish.pop(0))
        for i in range(3):
            bank_free[2 * i] = bank_free[2 * i + 1] = pair_free[i][-1]
        phase_end()

        got = load[6].start(sp, woraw[:], wo)
        pool.wait(got)
        hi = pool.do(TENSOR_COPY, Woh[:], woraw[:])
        pool.wait(hi)
        w_ready = pool.do(TENSOR_TENSOR, Wol[:], woraw[:], Woh[:], ALU.subtract)
        for t in range(NT):
            _, ready = to_columns(t, qtok[:, t, :], None, 4 + t % 4, [])
            ts = slice(t * P, (t + 1) * P)
            bk = t % 4
            pe.wait(ready, w_ready, bank_free[bk])
            for c in range(DC):
                done = mm3(PS[:, bk, :], xTh[:, c, ts], xTl[:, c, ts], Woh[:, c, :], Wol[:, c, :], c == 0, c == DC - 1)
            dve.wait(done)
            bank_free[bk] = X_ready[t // TPG] = dve.do(TENSOR_TENSOR, X[:, t, :], PS[:, bk, :], X[:, t, :], ALU.add)
        phase_end()

    ffn(0)
    phase_end()
    attention()
    ffn(1)
    for o in out_x:
        sp.wait((o.sem, o.count))

    block = ctx.enter_context(nc.Block())

    @block.sync
    def _(e):
        sp.emit(e)

    @block.tensor
    def _(e):
        pe.emit(e)

    @block.scalar
    def _(e):
        act.emit(e)

    @block.vector
    def _(e):
        dve.emit(e)

    @block.gpsimd
    def _(e):
        pool.emit(e)


def shape_constants():
    ident = np.eye(P, dtype=np.float32)
    sel = np.zeros((P, NCH * P), np.float32)
    for e in range(E):
        for part in range(3):
            sel[part * E + e, FS + e * F:FS + (e + 1) * F] = 1.0
    sel[3 * E, :FS] = 1.0
    inv = (1.0 / np.float32(10000.0) ** (np.arange(0, HD, 2, dtype=np.float32) / np.float32(HD))).astype(np.float32)
    ang = np.arange(S, dtype=np.float32)[:, None] * inv[None, :]
    cos = np.cos(ang).astype(np.float32)
    sin = np.sin(ang).astype(np.float32)
    rope = np.stack([np.concatenate([cos, cos], 1), np.concatenate([-sin, sin], 1)], 1)
    rope = np.ascontiguousarray(rope.reshape(QT, P, 2, HD).transpose(1, 0, 2, 3))
    return ident, sel, rope


def kernel(**inputs):
    from contextlib import ExitStack
    import ml_dtypes
    import concourse.bacc as bacc
    from concourse.bass_utils import run_bass_kernel_spmd

    a = {k: np.asarray(v) for k, v in inputs.items()}
    w1 = np.concatenate([a["L0_ffn_sw1"], a["L0_ffn_rw1"].transpose(1, 0, 2).reshape(D, E * F)], axis=1)
    w3 = np.concatenate([a["L0_ffn_sw3"], a["L0_ffn_rw3"].transpose(1, 0, 2).reshape(D, E * F)], axis=1)
    w2 = np.concatenate([a["L0_ffn_sw2"], a["L0_ffn_rw2"].reshape(E * F, D)], axis=0)
    pad = NCH * P - HID

    def columns(w):
        w = np.pad(w, ((0, 0), (0, pad)))
        return w.reshape(DC, P, NCH, P).transpose(2, 1, 0, 3).reshape(NCH, P, D)

    ffn_w = np.concatenate([columns(w1), columns(w3), np.pad(w2, ((0, pad), (0, 0))).reshape(NCH, P, D)], axis=2)

    def rows(w):
        return w.reshape(DC, P, -1).transpose(1, 0, 2)

    ident, sel, rope = shape_constants()
    arrays = {
        "x": a["L0_attn_x"].reshape(TOK, D),
        "ffn_w": ffn_w,
        "gate_w": rows(a["L0_ffn_gate_w"]),
        "wqkv": rows(np.concatenate([a["L0_attn_Wq"], a["L0_attn_Wk"], a["L0_attn_Wv"]], axis=0).T),
        "wo": rows(a["L0_attn_Wo"].T),
        "sel": sel.astype(ml_dtypes.bfloat16),
        "rope": rope,
        "ident": ident,
    }
    arrays = {k: np.ascontiguousarray(v) for k, v in arrays.items()}
    nc = bacc.Bacc("TRN2", target_bir_lowering=False, num_devices=1)
    args = {k: nc.dram_tensor(k, v.shape, mybir.dt.from_np(v.dtype), kind="ExternalInput").ap()
            for k, v in arrays.items()}
    out = nc.dram_tensor("y", (TOK, D), F32, kind="ExternalOutput").ap()
    with ExitStack() as ctx:
        macaron(nc, ctx, out=out, **args)
    got = run_bass_kernel_spmd(nc, [arrays], core_ids=[0])
    return got.results[0]["y"].reshape(B, S, D)
```

```python
import numpy as np

import concourse.bass as bass
from concourse import mybir

P = 128
B, S, D = 2, 1024, 512
TOK = B * S
NT = TOK // P
DC = D // P
GRP = 512
NG = TOK // GRP
TPG = GRP // P
F, E, N_SHARED = 352, 8, 2
FS = F * N_SHARED
HID = FS + E * F
NCH = -(-HID // P)
SUPER = 4
NSUP = NCH // SUPER
SHARED_ONLY = FS // P
WCOL = 2 * D + D
NH, NKV = 16, 4
HD = D // NH
REP = NH // NKV
QT = S // P
SCALE = float(HD) ** -0.5
EPS = 1e-5
RSQRT_BITS = float(0x5F3759DF)
STK = 3 * HD
ROWS = STK + 2
VCOL = 2 * HD + 1
RING = 5
PBUF = 4
LAG = 4

F32 = mybir.dt.float32
F32R = mybir.dt.float32r
BF16 = mybir.dt.bfloat16
I32 = mybir.dt.int32
ALU = mybir.AluOpType
ACT = mybir.ActivationFunctionType
AX = mybir.AxisListType


def ACTIVATION(e, *args, **kw):
    return e.activation(*args, **kw)


def BN_AGGR(e, *args, **kw):
    return e.bn_aggr(*args, **kw)


def BN_STATS(e, *args, **kw):
    return e.bn_stats(*args, **kw)


def MATCH_REPLACE(e, *args, **kw):
    return e.match_replace(*args, **kw)


def MATMUL(e, *args, **kw):
    return e.matmul(*args, **kw)


def MAX(e, *args, **kw):
    return e.max(*args, **kw)


def MEMSET(e, *args, **kw):
    return e.memset(*args, **kw)


def RECIPROCAL(e, *args, **kw):
    return e.reciprocal(*args, **kw)


def SCALAR_TENSOR_TENSOR(e, *args, **kw):
    return e.scalar_tensor_tensor(*args, **kw)


def TENSOR_COPY(e, *args, **kw):
    return e.tensor_copy(*args, **kw)


def TENSOR_REDUCE(e, *args, **kw):
    return e.tensor_reduce(*args, **kw)


def TENSOR_SCALAR(e, *args, **kw):
    return e.tensor_scalar(*args, **kw)


def TENSOR_TENSOR(e, *args, **kw):
    return e.tensor_tensor(*args, **kw)


def TRANSPOSE(e, *args, **kw):
    return e.transpose(*args, **kw)


class Queue:

    def __init__(self, nc, ctx, name):
        self.sem = ctx.enter_context(nc.semaphore(f"{name}_done"))
        self.todo, self.count, self.seen = [], 0, {}

    def do(self, instruction, *args, tick=True, **kw):
        if tick:
            self.count += 1
            self.todo.append(lambda e: instruction(e, *args, **kw).then_inc(self.sem, 1))
        else:
            self.todo.append(lambda e: instruction(e, *args, **kw))
        return (self.sem, self.count) if tick else None

    def wait(self, *events):
        for event in events:
            if event is None:
                continue
            sem, value = event
            if self.seen.get(id(sem), 0) < value:
                self.seen[id(sem)] = value
                self.todo.append(lambda e, s=sem, v=value: e.wait_ge(s, v))

    def last(self):
        return (self.sem, self.count)

    def emit(self, engine):
        for step in self.todo:
            step(engine)


class Landing:

    def __init__(self, nc, ctx, name):
        self.sem, self.count = ctx.enter_context(nc.semaphore(name)), 0

    def start(self, queue, out, in_):
        self.count += 16
        queue.todo.append(lambda e: e.dma_start(out, in_).then_inc(self.sem, 16))
        return (self.sem, self.count)


def macaron(nc, ctx, x, ffn_w, gate_w, wqkv, wo, sel, rope, ident, comb, out):
    def place(name, shape, dt, at):
        at = -(-at // 32) * 32
        end = at + int(np.prod(shape[1:])) * (2 if dt == BF16 else 4)
        assert end <= nc.sbuf_usable_end, (name, end - nc.sbuf_usable_end)
        return nc.alloc_sbuf_tensor_at(name, list(shape), dt, offset=at), end

    QKV = D + 2 * NKV * HD
    x_at = -(-nc.sbuf_base // 64) * 64
    X, at = place("X", (P, NT, D), F32, x_at)
    identf, at = place("identf", (P, P), F32, at)
    identb, at = place("identb", (P, P), BF16, at)
    combS, at = place("combS", (VCOL, HD + 1), F32, at)
    mv, at = place("mv", (P, NT, 2), F32, at)
    stats, at = place("stats", (P, 2, 6), F32, at)
    rstd, at = place("rstd", (P, NT), F32, at)
    ve, at = place("ve", (P, NT), F32, at)
    nwt, at = place("nwt", (P, NT), F32, at)
    xt_at = -(-at // 32) * 32
    xTh, at = place("xTh", (P, B, DC, S), F32R, xt_at)
    xTl, at = place("xTl", (P, B, DC, S), F32R, at)
    xn_at = at
    xn, at = place("xn", (P, 2, D), F32, at)
    arena = at

    raw, at = place("raw", (P, WCOL), F32, arena)
    W, at = place("W", (P, RING, 2, WCOL), F32R, at)
    silu, at = place("silu", (P, 2, GRP), F32, at)
    hid, at = place("hid", (P, 2, GRP), F32, at)
    hidh, at = place("hidh", (P, 2, GRP), F32R, at)
    hidl, at = place("hidl", (P, 2, GRP), F32R, at)
    selS, at = place("selS", (P, NCH * P), BF16, at)
    cwT, at = place("cwT", (P, TOK), BF16, at)
    gf, at = place("gf", (P, DC, E), F32, at)
    gh, at = place("gh", (P, DC, E), F32R, at)
    gl, at = place("gl", (P, DC, E), F32R, at)
    l16, at = place("l16", (P, NT, 2 * E), F32, at)
    r16, at = place("r16", (P, NT, 2 * E), F32, at)
    m8, at = place("m8", (P, NT, 8), F32, at)
    rmx, at = place("rmx", (P, NT), F32, at)
    rsm, at = place("rsm", (P, NT), F32, at)
    cw, at = place("cw", (P, NT, E), F32, at)
    cwb, at = place("cwb", (P, NT, P), BF16, at)

    KS, at = place("KS", (P, B, NKV, S), F32R, arena)
    V, at = place("V", (P, NT, NKV, VCOL), F32R, at)
    Wqkv, at = place("Wqkv", (P, 2, DC, QKV), F32R, at)
    qtok, at = place("qtok", (P, NT, D), F32, at)
    qtok_at = at - NT * D * 4
    OT, at = place("OT", (P, GRP), F32, at)
    wraw, _ = place("wraw", (P, DC, QKV), F32, qtok_at + (NT // 2) * D * 4)
    assert DC * QKV <= (NT // 2) * D
    qka, at = place("qka", (P, 2, NH + NKV, HD), F32, x_at)
    qkr, at = place("qkr", (P, 2, NH + NKV, HD), F32, at)
    kst, at = place("kst", (P, 2, NKV, STK), F32, at)
    ropeS, at = place("ropeS", (P, QT, 2, HD), F32, at)
    assert at <= x_at + 2 * TPG * D * 4
    Ph, at = place("Ph", (P, PBUF, 2 * GRP), F32R, x_at)
    Pl, at = place("Pl", (P, PBUF, 2 * GRP), F32R, at)
    assert at <= x_at + NT * D * 4
    TS, _ = place("TS", (P, 2, REP, STK), F32, xn_at)
    quarter = DC * S * 4
    QS = [place(f"QS{i}", (P, REP, S), F32R, xt_at + quarter * (0, 2, 1)[i])[0] for i in range(3)]
    PT, at = place("PT", (P, 3, 2 * GRP), F32, xt_at + 3 * quarter)
    nm, at = place("nm", (P, 3 * REP, 2 * QT), F32, at)
    nmf, at = place("nmf", (P, 3 * REP, QT), F32, at)
    MT, at = place("MT", (2 * QT, 2, P), F32, at)
    rL, at = place("rL", (P, 2, TPG), F32, at)
    assert at <= xn_at
    Wo, at = place("Wo", (P, 2, DC, D), F32R, arena + WCOL * 4 * (1 + 2 * (RING - 1)))
    woraw, at = place("woraw", (P, D), F32, at)
    assert at <= qtok_at

    PS = ctx.enter_context(nc.psum_tensor("PS", [P, 8, GRP], F32))
    x_home = nc.dram_tensor("x_home", (TOK, D), F32, kind="Internal").ap()

    pe, act, dve, pool, sp = (Queue(nc, ctx, n) for n in ("pe", "act", "dve", "pool", "sp"))
    in_id, in_comb, in_gate, in_sel, in_rope = (Landing(nc, ctx, n) for n in
                                                ("in_id", "in_comb", "in_gate", "in_sel", "in_rope"))
    in_raw = Landing(nc, ctx, "in_raw")
    in_wqkv = [Landing(nc, ctx, f"in_wqkv{c}") for c in range(DC)]
    in_wo = [Landing(nc, ctx, f"in_wo{c}") for c in range(3)]
    in_x = [Landing(nc, ctx, f"in_x{g}") for g in range(NG)]
    in_m = [Landing(nc, ctx, f"in_m{i}") for i in range(3 * REP)]
    out_home = [Landing(nc, ctx, f"out_home{g}") for g in range(NG)]
    out_x = [Landing(nc, ctx, f"out_x{g}") for g in range(NG)]
    bank_free = [None] * 8

    def mm3(dst, lh, ll, rh, rl, first, last):
        pe.do(MATMUL, dst, lh, rh, start=first, stop=False, tick=False)
        pe.do(MATMUL, dst, lh, rl, start=False, stop=False, tick=False)
        return pe.do(MATMUL, dst, ll, rh, start=False, stop=last, tick=last)

    def group_rows(dram, g):
        return dram[g * GRP:(g + 1) * GRP, :].rearrange("(t p) d -> p t d", p=P)

    def group_of_X(g):
        return X[:, g * TPG:(g + 1) * TPG, :]

    def tile_columns(t):
        return t // QT, slice((t % QT) * P, (t % QT + 1) * P)

    id_in = in_id.start(sp, identf[:], ident)
    X_ready = [in_x[g].start(sp, group_of_X(g), group_rows(x, g)) for g in range(NG)]
    comb_in = in_comb.start(sp, combS[:], comb)
    dve.wait(id_in)
    identb_ready = dve.do(TENSOR_COPY, identb[:], identf[:])

    def to_columns(t, src, src_ready, bank):
        b, cols = tile_columns(t)
        pe.wait(src_ready, bank_free[bank], id_in)
        for c in range(DC):
            turned = pe.do(TRANSPOSE, PS[:, bank, c * P:(c + 1) * P], src[:, c * P:(c + 1) * P], identf[:],
                           tick=(c == DC - 1))
        tile = PS[:, bank, :].rearrange("p (c n) -> p c n", c=DC)
        act.wait(turned)
        hi = act.do(ACTIVATION, xTh[:, b, :, cols], tile, ACT.Copy)
        dve.wait(turned, hi)
        lo = dve.do(TENSOR_TENSOR, xTl[:, b, :, cols], tile, xTh[:, b, :, cols], ALU.subtract)
        bank_free[bank] = lo
        return turned, lo

    xn_free = [None, None]

    def layer_norm(g, ready, banks):
        ts = slice(g * TPG, (g + 1) * TPG)
        tiles = range(g * TPG, (g + 1) * TPG)
        dve.wait(X_ready[g])
        st = [None, None]
        for t in tiles:
            st[t % 2] = dve.do(BN_STATS, stats[:, t % 2, :], X[:, t, :])
            dve.wait(st[t % 2])
            done = dve.do(BN_AGGR, mv[:, t, :], stats[:, t % 2, :])
        dve.wait(done)
        r = dve.do(TENSOR_SCALAR, ve[:, ts], mv[:, ts, 1], EPS, None, ALU.add)
        dve.wait(r)
        r = dve.do(TENSOR_SCALAR, rstd[:, ts].bitcast(I32), ve[:, ts].bitcast(I32), -0.5, RSQRT_BITS,
                   ALU.mult, ALU.add)
        for step in range(4):
            if step == 2:
                yield
            for p, q in ((rstd, rstd), (nwt, ve)):
                dve.wait(r)
                r = dve.do(TENSOR_TENSOR, nwt[:, ts], p[:, ts], q[:, ts], ALU.mult)
            dve.wait(r)
            r = dve.do(TENSOR_SCALAR, nwt[:, ts], nwt[:, ts], -0.5, 1.5, ALU.mult, ALU.add)
            dve.wait(r)
            r = dve.do(TENSOR_TENSOR, rstd[:, ts], rstd[:, ts], nwt[:, ts], ALU.mult)
        dve.wait(r)
        waiting = None
        for t in tiles:
            dve.wait(xn_free[t % 2])
            n = dve.do(TENSOR_SCALAR, xn[:, t % 2, :], X[:, t, :], mv[:, t, 0:1], rstd[:, t:t + 1],
                       ALU.subtract, ALU.mult)
            if waiting:
                yield
                xn_free[waiting[0] % 2], _ = to_columns(*waiting, banks[waiting[0] % len(banks)])
            waiting = (t, xn[:, t % 2, :], n)
        yield
        xn_free[t % 2], ready[g] = to_columns(*waiting, banks[t % len(banks)])

    def finish(steps):
        for _ in steps:
            pass

    def ffn(x_ready, norm, arena_free, before_group, after_group):
        w_ready, w_free, raw_free = [None] * NCH, [None] * RING, [None]

        def weights(k):
            sp.wait(raw_free[0])
            got = in_raw.start(sp, raw[:], ffn_w[k])
            s = k % RING
            pool.wait(got, w_free[s])
            hi = pool.do(TENSOR_COPY, W[:, s, 0, :], raw[:])
            pool.wait(hi)
            raw_free[0] = w_ready[k] = pool.do(TENSOR_TENSOR, W[:, s, 1, :], raw[:], W[:, s, 0, :], ALU.subtract)

        for k in range(RING - 1):
            weights(k)
        yield
        sp.wait(*arena_free())
        pool.wait(*arena_free())
        got_gate = in_gate.start(sp, gf[:], gate_w)
        got_sel = in_sel.start(sp, selS[:], sel)
        weights(RING - 1)
        pool.wait(got_gate)
        g1 = pool.do(TENSOR_COPY, gh[:], gf[:])
        pool.wait(g1)
        gate_ready = pool.do(TENSOR_TENSOR, gl[:], gf[:], gh[:], ALU.subtract)
        pad_ready = pool.do(MEMSET, l16[:], -1.0)
        z = pool.do(MEMSET, cwb[:], 0.0)
        pool.wait(z)
        ones_ready = pool.do(MEMSET, cwb[:, :, 3 * E:3 * E + 1], 1.0)
        cw_ready = [None]
        BG = 7

        def router():
            pe.wait(gate_ready, x_ready[NG - 1], bank_free[BG])
            for t in range(NT):
                dst = PS[:, BG, t * E:(t + 1) * E]
                b, cols = tile_columns(t)
                for c in range(DC):
                    logits = mm3(dst, xTh[:, b, c, cols], xTl[:, b, c, cols], gh[:, c, :], gl[:, c, :],
                                 c == 0, c == DC - 1)
                if t % TPG == TPG - 1:
                    yield
            lg = PS[:, BG, 0:NT * E].rearrange("p (t e) -> p t e", e=E)
            dve.wait(logits)
            r = dve.do(TENSOR_REDUCE, rmx[:], lg, AX.X, ALU.max)
            dve.wait(r, pad_ready)
            r = dve.do(TENSOR_TENSOR, l16[:, :, 0:E], lg, rmx[:].unsqueeze(2).broadcast_to([P, NT, E]), ALU.subtract)
            bank_free[BG] = r
            act.wait(r)
            r = act.do(ACTIVATION, l16[:, :, 0:E], l16[:, :, 0:E], ACT.Exp)
            yield
            dve.wait(r)
            r = dve.do(TENSOR_REDUCE, rsm[:], l16[:, :, 0:E], AX.X, ALU.add)
            dve.wait(r)
            dve.do(RECIPROCAL, rsm[:], rsm[:])
            for t in range(NT):
                r = dve.do(MAX, m8[:, t, :], l16[:, t, :])
                if t == NT // 2:
                    yield
            dve.wait(r)
            r = dve.do(MEMSET, m8[:, :, 2:8], -1.0)
            yield
            dve.wait(r)
            for t in range(NT):
                r = dve.do(MATCH_REPLACE, r16[:, t, :], m8[:, t, :], l16[:, t, :], 0.0)
                if t == NT // 2:
                    yield
            dve.wait(r)
            r = dve.do(TENSOR_TENSOR, cw[:], l16[:, :, 0:E], r16[:, :, 0:E], ALU.subtract)
            dve.wait(r)
            r = dve.do(TENSOR_TENSOR, cw[:], cw[:], rsm[:].unsqueeze(2).broadcast_to([P, NT, E]), ALU.mult)
            yield
            dve.wait(ones_ready)
            for part in range(3):
                dve.wait(r)
                dst = cwb[:, :, part * E:(part + 1) * E]
                r = dve.do(TENSOR_COPY, dst, cw[:])
                if part < 2:
                    dve.wait(r)
                    r = dve.do(TENSOR_TENSOR, cw[:], cw[:], dst, ALU.subtract)
            HB = NT // 2
            for half in range(2):
                yield
                turned_to = PS[:, BG, :].bitcast(BF16).rearrange("p (t n) -> p t n", n=P)
                pe.wait(r, identb_ready, bank_free[BG])
                for i in range(HB):
                    tr = pe.do(TRANSPOSE, turned_to[:, i, :], cwb[:, half * HB + i, :], identb[:], tick=(i == HB - 1))
                dve.wait(tr)
                turned = bank_free[BG] = dve.do(TENSOR_COPY, cwT[:, half * HB * P:(half + 1) * HB * P],
                                                PS[:, BG, :].bitcast(BF16))
            cw_ready[0] = turned

        silu_free, hid_free = [None] * 2, [None] * 2
        Y_free = [bank_free[j] for j in range(TPG)]
        BANK_A, BANK_B, BANK_M = 4, 5, 6
        beside = []

        def second(item):
            k, c, g, s, i, ready = item
            pe.wait(ready)
            first, last = c == 0, c == SUPER - 1
            w2h, w2l = W[:, s, 0, 2 * D:], W[:, s, 1, 2 * D:]
            for j in range(TPG):
                if first:
                    pe.wait(Y_free[j])
                dst, js = PS[:, j, :], slice(j * P, (j + 1) * P)
                pe.do(MATMUL, dst, hidh[:, i, js], w2h, start=first, stop=False, tick=False)
                pe.do(MATMUL, dst, hidh[:, i, js], w2l, start=False, stop=False, tick=False)
                done = pe.do(MATMUL, dst, hidl[:, i, js], w2h, start=False, stop=last)
                if last:
                    t = g * TPG + j
                    dve.wait(done)
                    Y_free[j] = X_ready[g] = dve.do(SCALAR_TENSOR_TENSOR, X[:, t, :], dst, 0.5, X[:, t, :],
                                                    ALU.mult, ALU.add)
            hid_free[i] = done
            if last and k == NCH - 1:
                after_group(g, beside)
            if g == NG - 1:
                w_free[s] = done
                if k + RING < NCH:
                    weights(k + RING)

        def advance():
            if beside and next(beside[0], "end") == "end":
                beside.pop(0)

        pending, step = [], 0
        for sup in range(NSUP):
            for g in range(NG):
                gb, gs = g * GRP // S, slice(g * GRP % S, g * GRP % S + GRP)
                if sup == 0 and g == 0:
                    beside += [norm(n) for n in range(1, NG)] + [router()]
                while x_ready[g] is None:
                    advance()
                for c in range(SUPER):
                    k = sup * SUPER + c
                    s, i = k % RING, step % 2
                    step += 1
                    routed = k >= SHARED_ONLY
                    while routed and cw_ready[0] is None:
                        advance()
                    pe.wait(w_ready[k], x_ready[g])
                    for bank, col in ((BANK_A, 0), (BANK_B, D)):
                        pe.wait(bank_free[bank])
                        for d in range(DC):
                            ws = slice(col + d * P, col + (d + 1) * P)
                            done = mm3(PS[:, bank, :], W[:, s, 0, ws], W[:, s, 1, ws],
                                       xTh[:, gb, d, gs], xTl[:, gb, d, gs], d == 0, d == DC - 1)
                        if bank == BANK_A:
                            a_done = done
                    b_done = done
                    advance()
                    if routed:
                        pe.wait(cw_ready[0], got_sel, bank_free[BANK_M])
                        m_done = pe.do(MATMUL, PS[:, BANK_M, :], selS[:, k * P:(k + 1) * P],
                                       cwT[:, g * GRP:(g + 1) * GRP], start=True, stop=True)
                    act.wait(a_done, silu_free[i])
                    sl = bank_free[BANK_A] = act.do(ACTIVATION, silu[:, i, :], PS[:, BANK_A, :], ACT.Silu)
                    dve.wait(sl, b_done, hid_free[i])
                    h = dve.do(TENSOR_TENSOR, hid[:, i, :], silu[:, i, :], PS[:, BANK_B, :], ALU.mult)
                    bank_free[BANK_B] = silu_free[i] = h
                    if routed:
                        dve.wait(h, m_done)
                        h = bank_free[BANK_M] = dve.do(TENSOR_TENSOR, hid[:, i, :], hid[:, i, :],
                                                       PS[:, BANK_M, :], ALU.mult)
                    dve.wait(h)
                    h = dve.do(TENSOR_COPY, hidh[:, i, :], hid[:, i, :])
                    dve.wait(h)
                    h = dve.do(TENSOR_TENSOR, hidl[:, i, :], hid[:, i, :], hidh[:, i, :], ALU.subtract)
                    pending.append((k, c, g, s, i, h))
                    if len(pending) > 1:
                        second(pending.pop(0))
                    advance()
        second(pending.pop(0))
        while beside:
            advance()
        for j in range(TPG):
            bank_free[j] = Y_free[j]

    def attention(h_ready, home):
        ends = [q.last() for q in (pe, act, dve, pool)]
        for q in (pe, act, dve, pool, sp):
            q.wait(*ends)
        w_ready = []
        got = [in_wqkv[c].start(sp, wraw[:, c, :], wqkv[:, c, :]) for c in range(DC)]
        for c in range(DC):
            act.wait(got[c])
            hi = act.do(ACTIVATION, Wqkv[:, 0, c, :], wraw[:, c, :], ACT.Copy)
            dve.wait(hi, got[c])
            w_ready.append(dve.do(TENSOR_TENSOR, Wqkv[:, 1, c, :], wraw[:, c, :], Wqkv[:, 0, c, :], ALU.subtract))
        vones = pool.do(MEMSET, V[:, :, :, HD:HD + 1].bitcast(F32), 1.0)
        pool.wait(vones)
        ones = pool.do(MEMSET, KS[STK:ROWS, :, :, :].bitcast(F32), 1.0)
        sp.wait(*home)
        got_rope = in_rope.start(sp, ropeS[:], rope)
        for q in (act, dve, pool):
            q.wait(*home)

        half = HD // 2
        NQK = NH + NKV
        kst_free, qk_free = [None, None], [None, None]

        def project(t, banks):
            b, cols = tile_columns(t)
            bq = banks[0]
            pe.wait(h_ready[t // TPG], bank_free[bq], bank_free[bq + 1])
            for part, n0, n1 in ((0, 0, D), (1, D, QKV)):
                for c in range(DC):
                    pe.wait(w_ready[c])
                    done = mm3(PS[:, bq + part, 0:n1 - n0], xTh[:, b, c, cols], xTl[:, b, c, cols],
                               Wqkv[:, 0, c, n0:n1], Wqkv[:, 1, c, n0:n1], c == 0, c == DC - 1)
            i = t % 2
            qk = PS[:, bq:bq + 2, :].rearrange("p b n -> p (b n)")[:, 0:NQK * HD].rearrange("p (h d) -> p h d", d=HD)
            v = PS[:, bq + 1, NKV * HD:2 * NKV * HD].rearrange("p (h d) -> p h d", d=HD)
            cos = ropeS[:, t % QT, 0:1, :].broadcast_to([P, NQK, HD])
            sin = ropeS[:, t % QT, 1:2, :].broadcast_to([P, NQK, HD])
            dve.wait(done, got_rope, qk_free[i])
            dve.do(TENSOR_TENSOR, qkr[:, i, :, 0:half], qk[:, :, half:], sin[:, :, 0:half], ALU.mult)
            dve.do(TENSOR_TENSOR, qkr[:, i, :, half:], qk[:, :, 0:half], sin[:, :, half:], ALU.mult)
            r = dve.do(TENSOR_TENSOR, qka[:, i, :, :], qk, cos, ALU.mult)
            act.wait(r, ones)
            return t, v, r, bq, act.do(ACTIVATION, V[:, t, :, 0:HD], v, ACT.Copy)

        def rotate(t, v, products, bq, v_hi):
            i = t % 2
            dve.wait(v_hi)
            bank_free[bq] = bank_free[bq + 1] = dve.do(TENSOR_TENSOR, V[:, t, :, HD + 1:], v, V[:, t, :, 0:HD],
                                                       ALU.subtract)
            dve.wait(products)
            k = dve.do(TENSOR_TENSOR, qka[:, i, NH:, :], qka[:, i, NH:, :], qkr[:, i, NH:, :], ALU.add)
            dve.do(TENSOR_TENSOR, qtok[:, t, :].rearrange("p (h d) -> p h d", d=HD),
                   qka[:, i, 0:NH, :], qkr[:, i, 0:NH, :], ALU.add)
            dve.wait(k, kst_free[i])
            hi = dve.do(TENSOR_COPY, kst[:, i, :, 0:HD].bitcast(F32R), qka[:, i, NH:, :])
            dve.wait(hi)
            dve.do(TENSOR_COPY, kst[:, i, :, HD:2 * HD], kst[:, i, :, 0:HD])
            qk_free[i] = dve.do(TENSOR_TENSOR, kst[:, i, :, 2 * HD:].bitcast(F32R), qka[:, i, NH:, :],
                                kst[:, i, :, 0:HD], ALU.subtract)
            return t, qk_free[i]

        def turn_keys(t, ready):
            b, cols = tile_columns(t)
            bk = 6
            pe.wait(ready, bank_free[bk])
            for h in range(NKV):
                tr = pe.do(TRANSPOSE, PS[0:STK, bk, h * P:(h + 1) * P], kst[:, t % 2, h, :], identf[:],
                           tick=(h == NKV - 1))
            kst_free[t % 2] = tr
            act.wait(tr)
            keys_ready[b] = bank_free[bk] = act.do(ACTIVATION, KS[0:STK, b, :, cols],
                                                   PS[0:STK, bk, :].rearrange("p (h n) -> p h n", n=P), ACT.Copy)

        keys_ready = [None, None]
        groups = [(b, g) for b in range(B) for g in range(NKV)]
        MISC, OB = 7, 6
        ts_free, mt_free = [None, None], [None, None]
        q_ready, m_ready = {}, {}
        pair_free, pairs, turn, stacks = {}, [], [0], [0]

        def stack_queries(n, t):
            b, g = groups[n]
            tile, i = b * QT + t, stacks[0] % 2
            stacks[0] += 1
            src = qtok[:, tile, g * REP * HD:(g + 1) * REP * HD].rearrange("p (h d) -> p h d", d=HD)
            dve.wait(ts_free[i])
            r = dve.do(TENSOR_COPY, TS[:, i, :, 0:HD].bitcast(F32R), src)
            dve.wait(r)
            dve.do(TENSOR_COPY, TS[:, i, :, 2 * HD:], TS[:, i, :, 0:HD])
            r = dve.do(TENSOR_TENSOR, TS[:, i, :, HD:2 * HD].bitcast(F32R), src, TS[:, i, :, 0:HD], ALU.subtract)
            return n, t, i, r

        def turn_queries(n, t, i, ready):
            pe.wait(ready, bank_free[MISC])
            for h in range(REP):
                tr = pe.do(TRANSPOSE, PS[0:STK, MISC, h * P:(h + 1) * P], TS[:, i, h, :], identf[:],
                           tick=(h == REP - 1))
            ts_free[i] = tr
            act.wait(tr)
            q_ready[(n, t)] = bank_free[MISC] = act.do(
                ACTIVATION, QS[n % 3][0:STK, :, t * P:(t + 1) * P],
                PS[0:STK, MISC, :].rearrange("p (h n) -> p h n", n=P), ACT.Copy)

        def take_pair():
            i = pairs[turn[0] % len(pairs)]
            turn[0] += 1
            pe.wait(pair_free.get(i))
            return i

        def row_max(n, h, t):
            b, g = groups[n]
            s = (n % 3) * REP + h
            i = take_pair()
            pe.wait(q_ready[(n, t)], keys_ready[b])
            for hf in range(2):
                done = pe.do(MATMUL, PS[:, i + hf, :], QS[n % 3][0:STK, h, t * P:(t + 1) * P],
                             KS[0:STK, b, g, hf * GRP:(hf + 1) * GRP], start=True, stop=True, tick=(hf == 1))
            dve.wait(done)
            pair_free[i] = dve.do(TENSOR_REDUCE, nmf[:, s, t:t + 1], PS[:, i:i + 2, :].rearrange("p b n -> p (b n)"),
                                  AX.X, ALU.max, negate=True)

        def split_max(n, h):
            s = (n % 3) * REP + h
            dve.wait(dve.last())
            hi = dve.do(TENSOR_COPY, nm[:, s, 0:QT].bitcast(F32R), nmf[:, s, :])
            dve.wait(hi)
            return n, h, dve.do(TENSOR_TENSOR, nm[:, s, QT:].bitcast(F32R), nmf[:, s, :], nm[:, s, 0:QT], ALU.subtract)

        def place_max(n, h, ready):
            s, j = (n % 3) * REP + h, h % 2
            pe.wait(ready, bank_free[MISC])
            tr = pe.do(TRANSPOSE, PS[0:2 * QT, MISC, 0:P], nm[:, s, :], identf[:])
            act.wait(tr, mt_free[j])
            bank_free[MISC] = r = act.do(ACTIVATION, MT[:, j, :], PS[0:2 * QT, MISC, 0:P], ACT.Copy)
            sp.wait(r)
            for part in range(2):
                m_ready[(n, h)] = mt_free[j] = in_m[s].start(
                    sp, QS[n % 3][STK + part:STK + part + 1, h, :].bitcast(F32).rearrange("p (t n) -> p t n", n=P),
                    MT[part * QT:(part + 1) * QT, j, :])

        pt_free, p_free, ot_free, rl_free = [None] * 3, [None] * PBUF, [None], [0]

        def scores(n, h, hf, pair, u):
            b, g = groups[n]
            i = take_pair()
            pe.wait(m_ready[(n, h)])
            for j in range(2):
                kt = 2 * pair + j
                done = pe.do(MATMUL, PS[:, i + j, :], KS[0:ROWS, b, g, kt * P:(kt + 1) * P],
                             QS[n % 3][0:ROWS, h, hf * GRP:(hf + 1) * GRP], start=True, stop=True, tick=(j == 1))
            act.wait(done, pt_free[u % 3])
            pair_free[i] = act.do(ACTIVATION, PT[:, u % 3, :], PS[:, i:i + 2, :].rearrange("p b n -> p (b n)"),
                                  ACT.Exp, scale=SCALE)
            return dict(n=n, h=h, hf=hf, pair=pair, u=u, ready=pair_free[i])

        def split_hi(w):
            u = w["u"]
            q, op, extra = (dve, TENSOR_COPY, ()) if hi_on_vector(w) else (act, ACTIVATION, (ACT.Copy,))
            q.wait(w["ready"], p_free[u % PBUF])
            w["ready"] = q.do(op, Ph[:, u % PBUF, :], PT[:, u % 3, :], *extra)

        def split_lo(w):
            u = w["u"]
            q = dve if lo_on_vector(w) else pool
            q.wait(w["ready"], p_free[u % PBUF])
            w["ready"] = pt_free[u % 3] = q.do(TENSOR_TENSOR, Pl[:, u % PBUF, :], PT[:, u % 3, :],
                                               Ph[:, u % PBUF, :], ALU.subtract)

        def hi_on_vector(w):
            return w["u"] % 4 == 1 or w["n"] == len(groups) - 1 and w["u"] % 4 == 3

        def lo_on_vector(w):
            return w["u"] % 4 == 2 or w["n"] == len(groups) - 1 and w["u"] % 4 != 0

        def values(w):
            n, h, hf, pair, u = (w[k] for k in ("n", "h", "hf", "pair", "u"))
            b, g = groups[n]
            pe.wait(w["ready"])
            if pair == 0:
                pe.wait(bank_free[OB])
            for j in range(2):
                kt = 2 * pair + j
                for k, part in enumerate((Ph, Pl)):
                    done = pe.do(MATMUL, PS[0:VCOL, OB, :], V[:, b * QT + kt, g, :],
                                 part[:, u % PBUF, j * GRP:(j + 1) * GRP],
                                 start=(kt == 0 and k == 0), stop=(kt == QT - 1 and k == 1), tick=(k == 1))
            p_free[u % PBUF] = done
            if pair == QT // 2 - 1:
                act.wait(done, ot_free[0])
                bank_free[OB] = r = act.do(ACTIVATION, OT[0:VCOL, :], PS[0:VCOL, OB, :], ACT.Copy)
                outputs.append((n, h, hf, r))

        def store_head(n, h, hf, r):
            b, g = groups[n]
            pe.wait(r, bank_free[MISC], comb_in)
            C = HD + 1
            for j in range(TPG):
                tr = pe.do(MATMUL, PS[:, MISC, j * C:(j + 1) * C], OT[0:VCOL, j * P:(j + 1) * P], combS[:],
                           start=True, stop=True, tick=(j == TPG - 1))
            ot_free[0] = tr
            o = PS[:, MISC, 0:TPG * C].rearrange("p (j w) -> p j w", w=C)
            q = rl_free[0] % 2
            rl_free[0] += 1
            dve.wait(tr)
            r = dve.do(RECIPROCAL, rL[:, q, :], o[:, :, HD])
            dve.wait(r)
            t0, c0 = b * QT + hf * TPG, (g * REP + h) * HD
            bank_free[MISC] = dve.do(TENSOR_TENSOR, qtok[:, t0:t0 + TPG, c0:c0 + HD], o[:, :, 0:HD],
                                     rL[:, q, :].unsqueeze(2).broadcast_to([P, TPG, HD]), ALU.mult)

        projected, rotated, stacked = [], [], []
        for t in range(NT + 2):
            if t < NT:
                projected.append(project(t, ((t % 2) * 2,) if t < QT else (0,)))
            while projected and (len(projected) > 1 or t >= QT):
                rotated.append(rotate(*projected.pop(0)))
                if len(rotated) > 1:
                    turn_keys(*rotated.pop(0))
            while rotated and t >= NT:
                turn_keys(*rotated.pop(0))
            if t == QT:
                while rotated:
                    turn_keys(*rotated.pop(0))
                pairs[:] = [2, 4]
                for i in pairs:
                    pair_free[i] = bank_free[i]
                pe.wait(bank_free[2], bank_free[3], bank_free[4], bank_free[5])
            if QT <= t < NT:
                for n in range(2):
                    stacked.append(stack_queries(n, t - QT))
                    if len(stacked) > 1:
                        turn_queries(*stacked.pop(0))
                if t == NT - 1:
                    turn_queries(*stacked.pop(0))
                for tq in ([t - QT - 1] if t > QT else []) + ([QT - 1] if t == NT - 1 else []):
                    for h in range(REP):
                        row_max(0, h, tq)
        for h in range(REP):
            place_max(*split_max(0, h))
        pairs[:] = [0, 2, 4]
        pair_free[0] = bank_free[0]
        pe.wait(bank_free[0], bank_free[1])

        work, outputs, maxima = [], [], []
        u = 0
        for n in range(len(groups)):
            for un in range(2 * REP * (QT // 2)):
                h, hf, pair = un // QT, un // (QT // 2) % 2, un % (QT // 2)
                if work:
                    split_hi(work[-1])
                    if not lo_on_vector(work[-1]):
                        split_lo(work[-1])
                work.append(scores(n, h, hf, pair, u))
                if n + 1 < len(groups):
                    row_max(n + 1, un // QT, un % QT)
                if maxima:
                    place_max(*maxima.pop(0))
                if n + 1 < len(groups) and un % QT == QT - 1:
                    maxima.append(split_max(n + 1, un // QT))
                if len(work) > 1 and lo_on_vector(work[-2]):
                    split_lo(work[-2])
                if work[0]["u"] == u - LAG:
                    values(work.pop(0))
                if outputs and pair == 0:
                    store_head(*outputs.pop(0))
                if stacked:
                    turn_queries(*stacked.pop(0))
                if n + 2 < len(groups) and un % 4 == 2:
                    stacked.append(stack_queries(n + 2, un // 4))
                u += 1
            if maxima:
                place_max(*maxima.pop(0))
        split_hi(work[-1])
        for w in work[-2:]:
            if lo_on_vector(w) or w is work[-1]:
                split_lo(w)
        store_head(*outputs.pop(0))
        for w in work:
            values(w)
        store_head(*outputs.pop(0))
        for i in (0, 2, 4):
            bank_free[i] = bank_free[i + 1] = pair_free[i]

    def project_out(loaded):
        w_ready, use = [], {}
        for c in range(DC):
            i = c % 3
            sp.wait(use.get(i))
            got = in_wo[i].start(sp, raw[:, i * D:(i + 1) * D], wo[:, c, :])
            act.wait(got)
            hi = act.do(ACTIVATION, Wo[:, 0, c, :], raw[:, i * D:(i + 1) * D], ACT.Copy)
            dve.wait(hi, got)
            use[i] = dve.do(TENSOR_TENSOR, Wo[:, 1, c, :], raw[:, i * D:(i + 1) * D], Wo[:, 0, c, :], ALU.subtract)
            w_ready.append(use[i])
        sp.wait(*w_ready)
        heads_ready = dve.last()
        turned = []
        for t in range(NT + 2):
            if t < NT:
                turned.append((t, to_columns(t, qtok[:, t, :], heads_ready, 4 + t % 4)[1]))
            if len(turned) > 2 or t >= NT:
                tt, ready = turned.pop(0)
                b, cols = tile_columns(tt)
                bk, g = tt % 4, tt // TPG
                pe.wait(ready, bank_free[bk])
                for c in range(DC):
                    pe.wait(w_ready[c])
                    done = mm3(PS[:, bk, :], xTh[:, b, c, cols], xTl[:, b, c, cols], Wo[:, 0, c, :], Wo[:, 1, c, :],
                               c == 0, c == DC - 1)
                dve.wait(done, loaded[g])
                bank_free[bk] = X_ready[g] = dve.do(TENSOR_TENSOR, X[:, tt, :], PS[:, bk, :], X[:, tt, :], ALU.add)
                if tt % TPG == TPG - 1:
                    yield g

    x1_ready, h_ready, x3_ready = [None] * NG, [None] * NG, [None] * NG
    home = [None] * NG

    def to_attention(g, beside):
        sp.wait(X_ready[g])
        home[g] = out_home[g].start(sp, group_rows(x_home, g), group_of_X(g))
        beside.append(layer_norm(g, h_ready, [7]))

    steps = ffn_steps = ffn(x1_ready, lambda g: layer_norm(g, x1_ready, [7]), lambda: (), None, to_attention)
    next(ffn_steps)
    finish(layer_norm(0, x1_ready, [4, 5, 6, 7]))
    finish(ffn_steps)

    attention(h_ready, home)

    loop_done = [q.last() for q in (pe, act, dve, pool)]
    for q in (act, pool, sp, dve, pe):
        q.wait(*loop_done)
    loaded = [in_x[g].start(sp, group_of_X(g), group_rows(x_home, g)) for g in range(NG)]
    projecting = project_out(loaded)
    second_ffn = ffn(x3_ready, lambda g: layer_norm(g, x3_ready, [7]), lambda: (pe.last(),), None,
                     lambda g, beside: (sp.wait(X_ready[g]),
                                        out_x[g].start(sp, group_rows(out, g), group_of_X(g))))
    g = next(projecting)
    next(second_ffn)
    for g in projecting:
        if g == NG - 1:
            finish(layer_norm(0, x3_ready, [4, 5, 6, 7]))
    finish(second_ffn)
    for o in out_x:
        sp.wait((o.sem, o.count))

    block = ctx.enter_context(nc.Block())

    @block.sync
    def _(e):
        sp.emit(e)

    @block.tensor
    def _(e):
        pe.emit(e)

    @block.scalar
    def _(e):
        act.emit(e)

    @block.vector
    def _(e):
        dve.emit(e)

    @block.gpsimd
    def _(e):
        pool.emit(e)


def shape_constants():
    ident = np.eye(P, dtype=np.float32)
    sel = np.zeros((P, NCH * P), np.float32)
    for e in range(E):
        for part in range(3):
            sel[part * E + e, FS + e * F:FS + (e + 1) * F] = 1.0
    sel[3 * E, :FS] = 1.0
    inv = (1.0 / np.float32(10000.0) ** (np.arange(0, HD, 2, dtype=np.float32) / np.float32(HD))).astype(np.float32)
    ang = np.arange(S, dtype=np.float32)[:, None] * inv[None, :]
    cos = np.cos(ang).astype(np.float32)
    sin = np.sin(ang).astype(np.float32)
    rope = np.stack([np.concatenate([cos, cos], 1), np.concatenate([-sin, sin], 1)], 1)
    rope = np.ascontiguousarray(rope.reshape(QT, P, 2, HD).transpose(1, 0, 2, 3))
    comb = np.zeros((VCOL, HD + 1), np.float32)
    comb[:HD + 1] = np.eye(HD + 1)
    comb[HD + 1:, :HD] = np.eye(HD)
    return ident, sel, rope, comb


def kernel(**inputs):
    from contextlib import ExitStack
    import ml_dtypes
    import concourse.bacc as bacc
    from concourse.bass_utils import run_bass_kernel_spmd

    a = {k: np.asarray(v) for k, v in inputs.items()}
    w1 = np.concatenate([a["L0_ffn_sw1"], a["L0_ffn_rw1"].transpose(1, 0, 2).reshape(D, E * F)], axis=1)
    w3 = np.concatenate([a["L0_ffn_sw3"], a["L0_ffn_rw3"].transpose(1, 0, 2).reshape(D, E * F)], axis=1)
    w2 = np.concatenate([a["L0_ffn_sw2"], a["L0_ffn_rw2"].reshape(E * F, D)], axis=0)
    pad = NCH * P - HID

    def columns(w):
        w = np.pad(w, ((0, 0), (0, pad)))
        return w.reshape(DC, P, NCH, P).transpose(2, 1, 0, 3).reshape(NCH, P, D)

    ffn_w = np.concatenate([columns(w1), columns(w3), np.pad(w2, ((0, pad), (0, 0))).reshape(NCH, P, D)], axis=2)

    def rows(w):
        return w.reshape(DC, P, -1).transpose(1, 0, 2)

    ident, sel, rope, comb = shape_constants()
    arrays = {
        "x": a["L0_attn_x"].reshape(TOK, D),
        "ffn_w": ffn_w,
        "gate_w": rows(a["L0_ffn_gate_w"]),
        "wqkv": rows(np.concatenate([a["L0_attn_Wq"], a["L0_attn_Wk"], a["L0_attn_Wv"]], axis=0).T),
        "wo": rows(a["L0_attn_Wo"].T),
        "sel": sel.astype(ml_dtypes.bfloat16),
        "rope": rope,
        "ident": ident,
        "comb": comb,
    }
    arrays = {k: np.ascontiguousarray(v) for k, v in arrays.items()}
    nc = bacc.Bacc("TRN2", target_bir_lowering=False, num_devices=1)
    args = {k: nc.dram_tensor(k, v.shape, mybir.dt.from_np(v.dtype), kind="ExternalInput").ap()
            for k, v in arrays.items()}
    out = nc.dram_tensor("y", (TOK, D), F32, kind="ExternalOutput").ap()
    with ExitStack() as ctx:
        macaron(nc, ctx, out=out, **args)
    got = run_bass_kernel_spmd(nc, [arrays], core_ids=[0])
    return got.results[0]["y"].reshape(B, S, D)
```

```python
import numpy as np

import concourse.bass as bass
from concourse import mybir

P = 128
B, S, D = 2, 1024, 512
TOK = B * S
NT = TOK // P
DC = D // P
GRP = 512
NG = TOK // GRP
TPG = GRP // P
F, E, N_SHARED = 352, 8, 2
FS = F * N_SHARED
HID = FS + E * F
NCH = -(-HID // P)
TAIL = HID - (NCH - 1) * P
SUPER = 4
NSUP = NCH // SUPER
SHARED_ONLY = FS // P
WCOL = 2 * D + D
NH, NKV = 16, 4
HD = D // NH
REP = NH // NKV
QT = S // P
SCALE = float(HD) ** -0.5
EPS = 1e-5
RSQRT_BITS = float(0x5F3759DF)
STK = 3 * HD
ROWS = STK + 2
VCOL = 2 * HD + 1
RING = 5
PTBUF = 4
PBUF = 4
LAG = 4

F32 = mybir.dt.float32
F32R = mybir.dt.float32r
BF16 = mybir.dt.bfloat16
I32 = mybir.dt.int32
ALU = mybir.AluOpType
ACT = mybir.ActivationFunctionType
AX = mybir.AxisListType


def ACTIVATION(e, *args, **kw):
    return e.activation(*args, **kw)


def BN_AGGR(e, *args, **kw):
    return e.bn_aggr(*args, **kw)


def BN_STATS(e, *args, **kw):
    return e.bn_stats(*args, **kw)


def MATCH_REPLACE(e, *args, **kw):
    return e.match_replace(*args, **kw)


def MATMUL(e, *args, **kw):
    return e.matmul(*args, **kw)


def MAX(e, *args, **kw):
    return e.max(*args, **kw)


def MEMSET(e, *args, **kw):
    return e.memset(*args, **kw)


def RECIPROCAL(e, *args, **kw):
    return e.reciprocal(*args, **kw)


def SCALAR_TENSOR_TENSOR(e, *args, **kw):
    return e.scalar_tensor_tensor(*args, **kw)


def TENSOR_COPY(e, *args, **kw):
    return e.tensor_copy(*args, **kw)


def TENSOR_REDUCE(e, *args, **kw):
    return e.tensor_reduce(*args, **kw)


def TENSOR_SCALAR(e, *args, **kw):
    return e.tensor_scalar(*args, **kw)


def TENSOR_TENSOR(e, *args, **kw):
    return e.tensor_tensor(*args, **kw)


def TRANSPOSE(e, *args, **kw):
    return e.transpose(*args, **kw)


class Queue:

    def __init__(self, nc, ctx, name):
        self.sem = ctx.enter_context(nc.semaphore(f"{name}_done"))
        self.todo, self.count, self.seen = [], 0, {}

    def do(self, instruction, *args, tick=True, **kw):
        if tick:
            self.count += 1
            self.todo.append(lambda e: instruction(e, *args, **kw).then_inc(self.sem, 1))
        else:
            self.todo.append(lambda e: instruction(e, *args, **kw))
        return (self.sem, self.count) if tick else None

    def wait(self, *events):
        for event in events:
            if event is None:
                continue
            sem, value = event
            if self.seen.get(id(sem), 0) < value:
                self.seen[id(sem)] = value
                self.todo.append(lambda e, s=sem, v=value: e.wait_ge(s, v))

    def last(self):
        return (self.sem, self.count)

    def emit(self, engine):
        for step in self.todo:
            step(engine)


class Landing:

    def __init__(self, nc, ctx, name):
        self.sem, self.count = ctx.enter_context(nc.semaphore(name)), 0

    def start(self, queue, out, in_):
        self.count += 16
        queue.todo.append(lambda e: e.dma_start(out, in_).then_inc(self.sem, 16))
        return (self.sem, self.count)


def macaron(nc, ctx, x, ffn_w, gate_w, wqkv, wo, sel, rope, ident, comb, out):
    def place(name, shape, dt, at):
        at = -(-at // 32) * 32
        end = at + int(np.prod(shape[1:])) * (2 if dt == BF16 else 4)
        assert end <= nc.sbuf_usable_end, (name, end - nc.sbuf_usable_end)
        return nc.alloc_sbuf_tensor_at(name, list(shape), dt, offset=at), end

    QKV = D + 2 * NKV * HD
    x_at = -(-nc.sbuf_base // 64) * 64
    X, at = place("X", (P, NT, D), F32, x_at)
    identf, at = place("identf", (P, P), F32, at)
    identb, at = place("identb", (P, P), BF16, at)
    combS, at = place("combS", (VCOL, E), F32, at)
    mv, at = place("mv", (P, NT, 2), F32, at)
    stats, at = place("stats", (P, 2, 6), F32, at)
    rstd, at = place("rstd", (P, NT), F32, at)
    ve, at = place("ve", (P, NT), F32, at)
    nwt, at = place("nwt", (P, NT), F32, at)
    xt_at = -(-at // 32) * 32
    xTh, at = place("xTh", (P, B, DC, S), F32R, xt_at)
    xTl, at = place("xTl", (P, B, DC, S), F32R, at)
    xn_at = at
    xn, at = place("xn", (P, 2, D), F32, at)
    arena = at

    first_raw = [place(f"raw{k}", (P, WCOL), F32, xt_at + (DC * S * (1 + 2 * (k // 2)) + WCOL * (k % 2)) * 4)[0]
                 for k in range(RING - 1)]
    assert 2 * WCOL <= DC * S

    raw, at = place("raw", (P, WCOL), F32, arena)
    W, at = place("W", (P, RING, 2, WCOL), F32R, at)
    silu, at = place("silu", (P, 2, GRP), F32, at)
    hid, at = place("hid", (P, 2, GRP), F32, at)
    hidh, at = place("hidh", (P, 2, GRP), F32R, at)
    hidl, at = place("hidl", (P, 2, GRP), F32R, at)
    selS, at = place("selS", (P, NCH * P), BF16, at)
    cwT, at = place("cwT", (P, TOK), BF16, at)
    gf, at = place("gf", (P, DC, E), F32, at)
    gw, at = place("gw", (P, DC, VCOL), F32R, at)
    LT, at = place("LT", (P, GRP), F32, at)
    l16, at = place("l16", (P, NT, 2 * E), F32, at)
    r16, at = place("r16", (P, NT, 2 * E), F32, at)
    m8, at = place("m8", (P, NT, 8), F32, at)
    rmx, at = place("rmx", (P, NT), F32, at)
    rsm, at = place("rsm", (P, NT), F32, at)
    cw, at = place("cw", (P, NT, E), F32, at)
    cwb, at = place("cwb", (P, NT, P), BF16, at)

    KS, at = place("KS", (P, B, NKV, S), F32R, arena)
    V, at = place("V", (P, NT, NKV, VCOL), F32R, at)
    wqkv_at = at
    Wqkv, at = place("Wqkv", (P, 2, DC, QKV), F32R, at)
    qtok, at = place("qtok", (P, NT, D), F32, at)
    qtok_at = at - NT * D * 4
    OT, _ = place("OT", (P, GRP), F32, at)
    ropeS, _ = place("ropeS", (P, QT, 2, HD), F32, at)
    SPARE = 1
    wraw, at = place("wraw", (P, DC, QKV), F32, arena + WCOL * 4 * (1 + 2 * SPARE))
    assert at <= arena + WCOL * 4 * (1 + 2 * (SPARE + 1)) and at <= arena + B * NKV * S * 4
    qka, at = place("qka", (P, 2, NH + NKV, HD), F32, x_at)
    qkr, at = place("qkr", (P, 2, NH + NKV, HD), F32, at)
    kst, at = place("kst", (P, 2, NKV, STK), F32, at)
    assert at <= x_at + 2 * TPG * D * 4
    Ph, at = place("Ph", (P, PBUF, 2 * GRP), F32R, x_at)
    Pl, at = place("Pl", (P, PBUF, 2 * GRP), F32R, at)
    assert at <= x_at + NT * D * 4
    TS, at = place("TS", (P, 2, REP, STK), F32, xn_at)
    nmf, at = place("nmf", (P, 3 * REP, QT), F32, at)
    assert at <= arena
    quarter = DC * S * 4
    QS = [place(f"QS{i}", (P, REP, S), F32R, xt_at + quarter * (0, 2, 1)[i])[0] for i in range(3)]
    PT, at = place("PT", (P, PTBUF, 2 * GRP), F32, xt_at + 3 * quarter)
    assert at <= xn_at
    nm, at = place("nm", (P, 3 * REP, 2 * QT), F32, wqkv_at)
    MT, at = place("MT", (2 * QT, 2, P), F32, at)
    rL, at = place("rL", (P, 2, TPG), F32, at)
    head, at = place("head", (P, 2, TPG, HD), F32, at)
    wo_at = arena + WCOL * 4 * (1 + 2 * (RING - 1))
    assert at <= wo_at
    Wo, at = place("Wo", (P, 2, DC, D), F32R, wo_at)
    woraw, at = place("woraw", (P, D), F32, at)
    assert at <= qtok_at

    PS = ctx.enter_context(nc.psum_tensor("PS", [P, 8, GRP], F32))
    x_home = nc.dram_tensor("x_home", (TOK, D), F32, kind="Internal").ap()

    pe, act, dve, pool, sp = (Queue(nc, ctx, n) for n in ("pe", "act", "dve", "pool", "sp"))
    in_id, in_comb, in_gate, in_sel, in_rope = (Landing(nc, ctx, n) for n in
                                                ("in_id", "in_comb", "in_gate", "in_sel", "in_rope"))
    in_raw = Landing(nc, ctx, "in_raw")
    in_first = [Landing(nc, ctx, f"in_first{k}") for k in range(RING - 1)]
    in_wqkv = [Landing(nc, ctx, f"in_wqkv{c}") for c in range(DC)]
    in_wo = Landing(nc, ctx, "in_wo")
    in_x = [Landing(nc, ctx, f"in_x{g}") for g in range(NG)]
    in_m = [Landing(nc, ctx, f"in_m{i}") for i in range(3 * REP)]
    out_home = [Landing(nc, ctx, f"out_home{g}") for g in range(NG)]
    out_x = [Landing(nc, ctx, f"out_x{g}") for g in range(NG)]
    bank_free = [None] * 8

    def mm3(dst, lh, ll, rh, rl, first, last):
        pe.do(MATMUL, dst, lh, rh, start=first, stop=False, tick=False)
        pe.do(MATMUL, dst, lh, rl, start=False, stop=False, tick=False)
        return pe.do(MATMUL, dst, ll, rh, start=False, stop=last, tick=last)

    def group_rows(dram, g):
        return dram[g * GRP:(g + 1) * GRP, :].rearrange("(t p) d -> p t d", p=P)

    def group_of_X(g):
        return X[:, g * TPG:(g + 1) * TPG, :]

    def tile_columns(t):
        return t // QT, slice((t % QT) * P, (t % QT + 1) * P)

    id_in = in_id.start(sp, identf[:], ident)
    X_ready = [in_x[g].start(sp, group_of_X(g), group_rows(x, g)) if g < NG // 2 else None for g in range(NG)]
    dve.wait(id_in)
    identb_ready = dve.do(TENSOR_COPY, identb[:], identf[:])

    def to_columns(t, src, src_ready, bank):
        b, cols = tile_columns(t)
        pe.wait(src_ready, bank_free[bank], id_in)
        for c in range(DC):
            turned = pe.do(TRANSPOSE, PS[:, bank, c * P:(c + 1) * P], src[:, c * P:(c + 1) * P], identf[:],
                           tick=(c == DC - 1))
        tile = PS[:, bank, :].rearrange("p (c n) -> p c n", c=DC)
        act.wait(turned)
        hi = act.do(ACTIVATION, xTh[:, b, :, cols], tile, ACT.Copy)
        dve.wait(turned, hi)
        lo = dve.do(TENSOR_TENSOR, xTl[:, b, :, cols], tile, xTh[:, b, :, cols], ALU.subtract)
        bank_free[bank] = lo
        return turned, lo

    xn_free = [None, None]

    def layer_norm(g, ready, banks):
        ts = slice(g * TPG, (g + 1) * TPG)
        tiles = range(g * TPG, (g + 1) * TPG)
        dve.wait(X_ready[g])
        st = [None, None]
        for t in tiles:
            if t == tiles[TPG // 2]:
                yield
            st[t % 2] = dve.do(BN_STATS, stats[:, t % 2, :], X[:, t, :])
            dve.wait(st[t % 2])
            done = dve.do(BN_AGGR, mv[:, t, :], stats[:, t % 2, :])
        dve.wait(done)
        r = dve.do(TENSOR_SCALAR, ve[:, ts], mv[:, ts, 1], EPS, None, ALU.add)
        dve.wait(r)
        r = dve.do(TENSOR_SCALAR, rstd[:, ts].bitcast(I32), ve[:, ts].bitcast(I32), -0.5, RSQRT_BITS,
                   ALU.mult, ALU.add)
        for step in range(4):
            if step == 2:
                yield
            for p, q in ((rstd, rstd), (nwt, ve)):
                dve.wait(r)
                r = dve.do(TENSOR_TENSOR, nwt[:, ts], p[:, ts], q[:, ts], ALU.mult)
            dve.wait(r)
            r = dve.do(TENSOR_SCALAR, nwt[:, ts], nwt[:, ts], -0.5, 1.5, ALU.mult, ALU.add)
            dve.wait(r)
            r = dve.do(TENSOR_TENSOR, rstd[:, ts], rstd[:, ts], nwt[:, ts], ALU.mult)
        dve.wait(r)
        waiting = None
        for t in tiles:
            dve.wait(xn_free[t % 2])
            n = dve.do(TENSOR_SCALAR, xn[:, t % 2, :], X[:, t, :], mv[:, t, 0:1], rstd[:, t:t + 1],
                       ALU.subtract, ALU.mult)
            if waiting:
                yield
                xn_free[waiting[0] % 2], _ = to_columns(*waiting, banks[waiting[0] % len(banks)])
            waiting = (t, xn[:, t % 2, :], n)
        yield
        xn_free[t % 2], ready[g] = to_columns(*waiting, banks[t % len(banks)])

    def finish(steps):
        for _ in steps:
            pass

    def ffn(x_ready, norm, arena_free, first_slot, landing, slot_left, after_group, beside):
        w_ready, w_free, raw_free = [None] * NCH, [None] * RING, [None]

        def slot(k):
            return (first_slot + k) % RING

        def weights(k):
            buffer, land = landing[k] if landing and k < RING - 1 else (raw, in_raw)
            if buffer is raw:
                sp.wait(raw_free[0])
            got = land.start(sp, buffer[:], ffn_w[k])
            s = slot(k)
            if buffer is raw or k >= 2:
                pool.wait(got, w_free[s])
                hi = pool.do(TENSOR_COPY, W[:, s, 0, :], buffer[:])
            else:
                act.wait(got)
                hi = act.do(ACTIVATION, W[:, s, 0, :], buffer[:], ACT.Copy)
            pool.wait(hi, got)
            w_ready[k] = pool.do(TENSOR_TENSOR, W[:, s, 1, :], buffer[:], W[:, s, 0, :], ALU.subtract)
            if buffer is raw:
                raw_free[0] = w_ready[k]

        def after_first_weights(steps):
            act.wait(w_ready[RING - 2])
            dve.wait(w_ready[RING - 2])
            yield from steps

        for k in range(RING - 1):
            weights(k)
        yield
        sp.wait(*arena_free())
        pool.wait(*arena_free())
        got_gate = in_gate.start(sp, gf[:], gate_w)
        got_sel = in_sel.start(sp, selS[:], sel)
        weights(RING - 1)
        pool.wait(got_gate)
        z = pool.do(MEMSET, gw[:].bitcast(F32), 0.0)
        pool.wait(z)
        hi = pool.do(TENSOR_COPY, gw[:, :, 0:E], gf[:])
        pool.wait(hi)
        gate_ready = pool.do(TENSOR_TENSOR, gw[:, :, HD + 1:HD + 1 + E], gf[:], gw[:, :, 0:E], ALU.subtract)
        pad_ready = pool.do(MEMSET, l16[:], -1.0)
        z = pool.do(MEMSET, cwb[:], 0.0)
        pool.wait(z)
        ones_ready = pool.do(MEMSET, cwb[:, :, 3 * E:3 * E + 1], 1.0)
        cw_ready, lt_free = [None] * NG, [None]
        BG = 7

        def router(g):
            ts, gb, gs = slice(g * TPG, (g + 1) * TPG), g * GRP // S, slice(g * GRP % S, g * GRP % S + GRP)
            pe.wait(gate_ready, x_ready[g], bank_free[BG])
            for d in range(DC):
                for part in (xTh, xTl):
                    r = pe.do(MATMUL, PS[0:VCOL, BG, :], gw[:, d, :], part[:, gb, d, gs],
                              start=(d == 0 and part is xTh), stop=(d == DC - 1 and part is xTl))
            act.wait(r, lt_free[0])
            bank_free[BG] = r = act.do(ACTIVATION, LT[0:VCOL, :], PS[0:VCOL, BG, :], ACT.Copy)
            yield
            pe.wait(r, comb_in)
            for j in range(TPG):
                r = pe.do(MATMUL, PS[:, BG, j * E:(j + 1) * E], LT[0:VCOL, j * P:(j + 1) * P], combS[:],
                          start=True, stop=True)
            lt_free[0] = r
            lg = PS[:, BG, 0:TPG * E].rearrange("p (t e) -> p t e", e=E)
            dve.wait(r)
            r = dve.do(TENSOR_REDUCE, rmx[:, ts], lg, AX.X, ALU.max)
            dve.wait(r, pad_ready)
            r = dve.do(TENSOR_TENSOR, l16[:, ts, 0:E], lg, rmx[:, ts].unsqueeze(2).broadcast_to([P, TPG, E]),
                       ALU.subtract)
            bank_free[BG] = r
            act.wait(r)
            r = act.do(ACTIVATION, l16[:, ts, 0:E], l16[:, ts, 0:E], ACT.Exp)
            yield
            dve.wait(r)
            r = dve.do(TENSOR_REDUCE, rsm[:, ts], l16[:, ts, 0:E], AX.X, ALU.add)
            dve.wait(r)
            dve.do(RECIPROCAL, rsm[:, ts], rsm[:, ts])
            for t in range(g * TPG, (g + 1) * TPG):
                r = dve.do(MAX, m8[:, t, :], l16[:, t, :])
            dve.wait(r)
            r = dve.do(MEMSET, m8[:, ts, 2:8], -1.0)
            dve.wait(r)
            for t in range(g * TPG, (g + 1) * TPG):
                r = dve.do(MATCH_REPLACE, r16[:, t, :], m8[:, t, :], l16[:, t, :], 0.0)
            yield
            dve.wait(r)
            r = dve.do(TENSOR_TENSOR, cw[:, ts], l16[:, ts, 0:E], r16[:, ts, 0:E], ALU.subtract)
            dve.wait(r)
            r = dve.do(TENSOR_TENSOR, cw[:, ts], cw[:, ts], rsm[:, ts].unsqueeze(2).broadcast_to([P, TPG, E]), ALU.mult)
            dve.wait(ones_ready)
            for part in range(3):
                dve.wait(r)
                dst = cwb[:, ts, part * E:(part + 1) * E]
                r = dve.do(TENSOR_COPY, dst, cw[:, ts])
                if part < 2:
                    dve.wait(r)
                    r = dve.do(TENSOR_TENSOR, cw[:, ts], cw[:, ts], dst, ALU.subtract)
            yield
            turned = PS[:, BG, 0:GRP // 2].bitcast(BF16)
            pe.wait(r, identb_ready, bank_free[BG])
            for j in range(TPG):
                r = pe.do(TRANSPOSE, turned[:, j * P:(j + 1) * P], cwb[:, g * TPG + j, :], identb[:])
            dve.wait(r)
            cw_ready[g] = bank_free[BG] = dve.do(TENSOR_COPY, cwT[:, g * GRP:(g + 1) * GRP], turned)

        silu_free, hid_free = [None] * 2, [None] * 2
        Y_free = [bank_free[j] for j in range(TPG)]
        BANK_A, BANK_B, BANK_M = 4, 5, 6
        def chunk_rows(k):
            return slice(0, P) if k < NCH - 1 else slice(P - TAIL, P)

        def owner(k):
            e, e_last = (k * P - FS) // F, (min((k + 1) * P, HID) - 1 - FS) // F
            return e if e == e_last else None

        def second(item):
            k, c, g, s, i, ready = item
            pe.wait(ready)
            first, last = c == 0, c == SUPER - 1
            rows = chunk_rows(k)
            w2h, w2l = W[rows, s, 0, 2 * D:], W[rows, s, 1, 2 * D:]
            for j in range(TPG):
                if first:
                    pe.wait(Y_free[j])
                dst, js = PS[:, j, :], slice(j * P, (j + 1) * P)
                pe.do(MATMUL, dst, hidh[rows, i, js], w2h, start=first, stop=False, tick=False)
                pe.do(MATMUL, dst, hidh[rows, i, js], w2l, start=False, stop=False, tick=False)
                done = pe.do(MATMUL, dst, hidl[rows, i, js], w2h, start=False, stop=last)
                if last:
                    t = g * TPG + j
                    dve.wait(done)
                    Y_free[j] = X_ready[g] = dve.do(SCALAR_TENSOR_TENSOR, X[:, t, :], dst, 0.5, X[:, t, :],
                                                    ALU.mult, ALU.add)
            hid_free[i] = done
            if last and k == NCH - 1:
                after_group(g, beside)
            if g == NG - 1:
                w_free[s] = done
                if k + RING < NCH:
                    weights(k + RING)
                if k + RING == NCH:
                    slot_left(done)

        def advance():
            if beside and next(beside[0], "end") == "end":
                beside.pop(0)

        pending, step = [], 0
        for sup in range(NSUP):
            for g in range(NG):
                gb, gs = g * GRP // S, slice(g * GRP % S, g * GRP % S + GRP)
                if sup == 0 and g == 0:
                    beside += [norm(n) for n in (1,) if x_ready[n] is None]
                    beside += [after_first_weights(norm(2)), norm(3)] + [router(n) for n in range(NG)]
                while x_ready[g] is None:
                    advance()
                for c in range(SUPER):
                    k = sup * SUPER + c
                    s, i = slot(k), step % 2
                    step += 1
                    routed = k >= SHARED_ONLY
                    while routed and cw_ready[g] is None:
                        advance()
                    pe.wait(w_ready[k], x_ready[g])
                    rows = chunk_rows(k)
                    w3_bank = BANK_B if k < NCH - 1 else BANK_A
                    for bank, col in ((BANK_A, 0), (BANK_B, D))[:1 + (w3_bank == BANK_B)]:
                        pe.wait(bank_free[bank])
                        for d in range(DC):
                            ws = slice(col + d * P, col + (d + 1) * P)
                            done = mm3(PS[:, bank, :], W[:, s, 0, ws], W[:, s, 1, ws],
                                       xTh[:, gb, d, gs], xTl[:, gb, d, gs], d == 0, d == DC - 1)
                        if bank == BANK_A:
                            a_done = done
                    b_done = done
                    advance()
                    if routed and (c == 0 or owner(k) is None or owner(k) != owner(k - 1)):
                        pe.wait(cw_ready[g], got_sel, bank_free[BANK_M])
                        m_done = pe.do(MATMUL, PS[:, BANK_M, :], selS[:, k * P:(k + 1) * P],
                                       cwT[:, g * GRP:(g + 1) * GRP], start=True, stop=True)
                    act.wait(a_done, silu_free[i])
                    sl = bank_free[BANK_A] = act.do(ACTIVATION, silu[rows, i, :], PS[0:rows.stop - rows.start, BANK_A, :],
                                                     ACT.Silu)
                    dve.wait(sl, b_done, hid_free[i])
                    h = dve.do(TENSOR_TENSOR, hid[rows, i, :], silu[rows, i, :], PS[rows, w3_bank, :], ALU.mult)
                    bank_free[w3_bank] = silu_free[i] = h
                    if routed:
                        dve.wait(h, m_done)
                        h = bank_free[BANK_M] = dve.do(TENSOR_TENSOR, hid[rows, i, :], hid[rows, i, :],
                                                       PS[rows, BANK_M, :], ALU.mult)
                    dve.wait(h)
                    h = dve.do(TENSOR_COPY, hidh[rows, i, :], hid[rows, i, :])
                    dve.wait(h)
                    h = dve.do(TENSOR_TENSOR, hidl[rows, i, :], hid[rows, i, :], hidh[rows, i, :], ALU.subtract)
                    pending.append((k, c, g, s, i, h))
                    if len(pending) > 1:
                        second(pending.pop(0))
                    advance()
        second(pending.pop(0))
        for j in range(TPG):
            bank_free[j] = Y_free[j]

    def attention(h_ready, home, wqkv_in, rope_in, beside):
        ends = [q.last() for q in (pe, act, dve, pool)]
        for q in (pe, act, dve, pool, sp):
            q.wait(*ends)
        w_ready = []
        for c in range(DC):
            act.wait(wqkv_in[c])
            hi = act.do(ACTIVATION, Wqkv[:, 0, c, :], wraw[:, c, :], ACT.Copy)
            dve.wait(hi, wqkv_in[c])
            w_ready.append(dve.do(TENSOR_TENSOR, Wqkv[:, 1, c, :], wraw[:, c, :], Wqkv[:, 0, c, :], ALU.subtract))
        vones = pool.do(MEMSET, V[:, :, :, HD:HD + 1].bitcast(F32), 1.0)
        pool.wait(vones, w_ready[-1])
        ones = pool.do(MEMSET, KS[STK:ROWS, :, :, :].bitcast(F32), 1.0)
        for q in (act, dve, pool):
            q.wait(*home[:NG // 2])

        half = HD // 2
        NQK = NH + NKV
        kst_free, qk_free = [None, None], [None, None]
        k_hi, k_dup, queries = {}, {}, {}

        def rotary(t, src, h0, h1, done):
            i, nh = t % 2, h1 - h0
            qk = src[:, 0:nh * HD].rearrange("p (h d) -> p h d", d=HD)
            cos = ropeS[:, t % QT, 0:1, :].broadcast_to([P, nh, HD])
            sin = ropeS[:, t % QT, 1:2, :].broadcast_to([P, nh, HD])
            dve.wait(done, rope_in, qk_free[i])
            dve.do(TENSOR_TENSOR, qkr[:, i, h0:h1, 0:half], qk[:, :, half:], sin[:, :, 0:half], ALU.mult)
            dve.do(TENSOR_TENSOR, qkr[:, i, h0:h1, half:], qk[:, :, 0:half], sin[:, :, half:], ALU.mult)
            return dve.do(TENSOR_TENSOR, qka[:, i, h0:h1, :], qk, cos, ALU.mult)

        def keys_and_values(t, bq, done):
            i = t % 2
            v = PS[:, bq + 1, NKV * HD:2 * NKV * HD].rearrange("p (h d) -> p h d", d=HD)
            act.wait(done, ones)
            v_hi = act.do(ACTIVATION, V[:, t, :, 0:HD], v, ACT.Copy)
            products = rotary(t, PS[:, bq + 1, :], NH, NH + NKV, v_hi)
            bank_free[bq + 1] = dve.do(TENSOR_TENSOR, V[:, t, :, HD + 1:], v, V[:, t, :, 0:HD], ALU.subtract)
            dve.wait(products)
            k = dve.do(TENSOR_TENSOR, qka[:, i, NH:, :], qka[:, i, NH:, :], qkr[:, i, NH:, :], ALU.add)
            act.wait(k, kst_free[i])
            k_hi[t] = act.do(ACTIVATION, kst[:, i, :, 0:HD].bitcast(F32R), qka[:, i, NH:, :], ACT.Copy)
            pool.wait(k_hi[t])
            k_dup[t] = pool.do(TENSOR_COPY, kst[:, i, :, HD:2 * HD], kst[:, i, :, 0:HD])

        def project(t, bq):
            b, cols = tile_columns(t)
            pe.wait(h_ready[t // TPG], bank_free[bq], bank_free[bq + 1])
            for part, n0, n1 in ((1, D, QKV), (0, 0, D)):
                for c in range(DC):
                    if part == 0 and c == 0:
                        keys_and_values(t, bq, done)
                    if c == DC // 2 or part == 0 and c == 0:
                        yield
                    pe.wait(w_ready[c])
                    done = mm3(PS[:, bq + part, 0:n1 - n0], xTh[:, b, c, cols], xTl[:, b, c, cols],
                               Wqkv[:, 0, c, n0:n1], Wqkv[:, 1, c, n0:n1], c == 0, c == DC - 1)
            products = rotary(t, PS[:, bq, :], 0, NH, done)
            bank_free[bq] = products
            i = t % 2
            pool.wait(products)
            queries[t] = qk_free[i] = pool.do(TENSOR_TENSOR, qtok[:, t, :].rearrange("p (h d) -> p h d", d=HD),
                                              qka[:, i, 0:NH, :], qkr[:, i, 0:NH, :], ALU.add)

        def split_keys(t):
            i = t % 2
            dve.wait(k_hi[t])
            return t, dve.do(TENSOR_TENSOR, kst[:, i, :, 2 * HD:].bitcast(F32R), qka[:, i, NH:, :],
                             kst[:, i, :, 0:HD], ALU.subtract)

        def turn_keys(t, ready):
            b, cols = tile_columns(t)
            bk = 6
            pe.wait(ready, k_dup[t], bank_free[bk])
            for h in range(NKV):
                tr = pe.do(TRANSPOSE, PS[0:STK, bk, h * P:(h + 1) * P], kst[:, t % 2, h, :], identf[:],
                           tick=(h == NKV - 1))
            kst_free[t % 2] = tr
            act.wait(tr)
            keys_ready[b] = bank_free[bk] = act.do(ACTIVATION, KS[0:STK, b, :, cols],
                                                   PS[0:STK, bk, :].rearrange("p (h n) -> p h n", n=P), ACT.Copy)

        keys_ready = [None, None]
        groups = [(b, g) for b in range(B) for g in range(NKV)]
        MISC, OB, SPARE_BANK = 7, 6, 4
        ts_free, mt_free = [None, None], [None, None]
        q_ready, m_ready = {}, {}
        pair_free, pairs, turn, stacks = {}, [], [0], [0]

        def stack_queries(n, t):
            b, g = groups[n]
            tile, i = b * QT + t, stacks[0] % 2
            stacks[0] += 1
            src = qtok[:, tile, g * REP * HD:(g + 1) * REP * HD].rearrange("p (h d) -> p h d", d=HD)
            (hi, op, extra), copy = ((act, ACTIVATION, (ACT.Copy,)), pool) if n < 2 else ((dve, TENSOR_COPY, ()), dve)
            hi.wait(queries[tile], ts_free[i])
            r = hi.do(op, TS[:, i, :, 0:HD].bitcast(F32R), src, *extra)
            copy.wait(r)
            dup = copy.do(TENSOR_COPY, TS[:, i, :, 2 * HD:], TS[:, i, :, 0:HD])
            dve.wait(r)
            r = dve.do(TENSOR_TENSOR, TS[:, i, :, HD:2 * HD].bitcast(F32R), src, TS[:, i, :, 0:HD], ALU.subtract)
            return n, t, i, dup, r

        def turn_queries(n, t, i, *ready):
            pe.wait(*ready, bank_free[MISC])
            for h in range(REP):
                tr = pe.do(TRANSPOSE, PS[0:STK, MISC, h * P:(h + 1) * P], TS[:, i, h, :], identf[:],
                           tick=(h == REP - 1))
            ts_free[i] = tr
            act.wait(tr)
            q_ready[(n, t)] = bank_free[MISC] = act.do(
                ACTIVATION, QS[n % 3][0:STK, :, t * P:(t + 1) * P],
                PS[0:STK, MISC, :].rearrange("p (h n) -> p h n", n=P), ACT.Copy)

        def take_pair():
            i = pairs[turn[0] % len(pairs)]
            turn[0] += 1
            pe.wait(pair_free.get(i))
            return i

        def row_max(n, h, t):
            b, g = groups[n]
            s = (n % 3) * REP + h
            i = take_pair()
            pe.wait(q_ready[(n, t)], keys_ready[b])
            for hf in range(2):
                done = pe.do(MATMUL, PS[:, i + hf, :], QS[n % 3][0:STK, h, t * P:(t + 1) * P],
                             KS[0:STK, b, g, hf * GRP:(hf + 1) * GRP], start=True, stop=True, tick=(hf == 1))
            dve.wait(done)
            pair_free[i] = dve.do(TENSOR_REDUCE, nmf[:, s, t:t + 1], PS[:, i:i + 2, :].rearrange("p b n -> p (b n)"),
                                  AX.X, ALU.max, negate=True)

        def split_max(n, h):
            s = (n % 3) * REP + h
            dve.wait(dve.last())
            hi = dve.do(TENSOR_COPY, nm[:, s, 0:QT].bitcast(F32R), nmf[:, s, :])
            dve.wait(hi)
            return n, h, dve.do(TENSOR_TENSOR, nm[:, s, QT:].bitcast(F32R), nmf[:, s, :], nm[:, s, 0:QT], ALU.subtract)

        def place_max(n, h, ready):
            s, j = (n % 3) * REP + h, h % 2
            pe.wait(ready, bank_free[MISC])
            tr = pe.do(TRANSPOSE, PS[0:2 * QT, MISC, 0:P], nm[:, s, :], identf[:])
            act.wait(tr, mt_free[j])
            bank_free[MISC] = r = act.do(ACTIVATION, MT[:, j, :], PS[0:2 * QT, MISC, 0:P], ACT.Copy)
            sp.wait(r)
            for part in range(2):
                m_ready[(n, h)] = mt_free[j] = in_m[s].start(
                    sp, QS[n % 3][STK + part:STK + part + 1, h, :].bitcast(F32).rearrange("p (t n) -> p t n", n=P),
                    MT[part * QT:(part + 1) * QT, j, :])

        pt_free, p_free, ot_free, rl_free = [None] * PTBUF, [None] * PBUF, [None], [0]

        def scores(n, h, hf, pair, u):
            b, g = groups[n]
            i = take_pair()
            pe.wait(m_ready[(n, h)])
            for j in range(2):
                kt = 2 * pair + j
                done = pe.do(MATMUL, PS[:, i + j, :], KS[0:ROWS, b, g, kt * P:(kt + 1) * P],
                             QS[n % 3][0:ROWS, h, hf * GRP:(hf + 1) * GRP], start=True, stop=True, tick=(j == 1))
            act.wait(done, pt_free[u % PTBUF])
            pair_free[i] = act.do(ACTIVATION, PT[:, u % PTBUF, :], PS[:, i:i + 2, :].rearrange("p b n -> p (b n)"),
                                  ACT.Exp, scale=SCALE)
            ob = SPARE_BANK if n == len(groups) - 1 and hf == 1 else OB
            return dict(n=n, h=h, hf=hf, pair=pair, u=u, ob=ob, ready=pair_free[i])

        def split_hi(w):
            u = w["u"]
            q, op, extra = (dve, TENSOR_COPY, ()) if hi_on_vector(w) else (act, ACTIVATION, (ACT.Copy,))
            q.wait(w["ready"], p_free[u % PBUF])
            w["ready"] = q.do(op, Ph[:, u % PBUF, :], PT[:, u % PTBUF, :], *extra)

        def split_lo(w):
            u = w["u"]
            q = dve if lo_on_vector(w) else pool
            q.wait(w["ready"], p_free[u % PBUF])
            w["ready"] = pt_free[u % PTBUF] = q.do(TENSOR_TENSOR, Pl[:, u % PBUF, :], PT[:, u % PTBUF, :],
                                               Ph[:, u % PBUF, :], ALU.subtract)

        def hi_on_vector(w):
            return w["u"] % 8 in (1, 3, 5) or w["n"] == len(groups) - 1 and w["u"] % 4 == 3

        def lo_on_vector(w):
            return w["u"] % 4 == 2 or w["n"] == len(groups) - 1 and w["u"] % 4 != 0

        def values(w):
            n, h, hf, pair, u, ob = (w[k] for k in ("n", "h", "hf", "pair", "u", "ob"))
            b, g = groups[n]
            pe.wait(w["ready"])
            if pair == 0:
                pe.wait(bank_free[ob])
            for j in range(2):
                kt = 2 * pair + j
                for k, part in enumerate((Ph, Pl)):
                    done = pe.do(MATMUL, PS[0:VCOL, ob, :], V[:, b * QT + kt, g, :],
                                 part[:, u % PBUF, j * GRP:(j + 1) * GRP],
                                 start=(kt == 0 and k == 0), stop=(kt == QT - 1 and k == 1), tick=(k == 1))
            p_free[u % PBUF] = done
            if pair == QT // 2 - 1:
                act.wait(done, ot_free[0])
                bank_free[ob] = r = act.do(ACTIVATION, OT[0:VCOL, :], PS[0:VCOL, ob, :], ACT.Copy)
                outputs.append((n, h, hf, r))

        def store_head(n, h, hf, r):
            b, g = groups[n]
            pe.wait(r, bank_free[MISC])
            for j in range(TPG):
                tr = pe.do(TRANSPOSE, PS[:, MISC, j * VCOL:(j + 1) * VCOL], OT[0:VCOL, j * P:(j + 1) * P],
                           identf[0:VCOL, 0:VCOL], tick=(j == TPG - 1))
            ot_free[0] = tr
            o = PS[:, MISC, 0:TPG * VCOL].rearrange("p (j w) -> p j w", w=VCOL)
            q = rl_free[0] % 2
            rl_free[0] += 1
            dve.wait(tr)
            dve.do(RECIPROCAL, rL[:, q, :], o[:, :, HD])
            r = dve.do(TENSOR_COPY, head[:, q, :, :], o[:, :, HD + 1:])
            dve.wait(r)
            bank_free[MISC] = r = dve.do(TENSOR_TENSOR, head[:, q, :, :], head[:, q, :, :], o[:, :, 0:HD], ALU.add)
            dve.wait(r)
            t0, c0 = b * QT + hf * TPG, (g * REP + h) * HD
            dve.do(TENSOR_TENSOR, qtok[:, t0:t0 + TPG, c0:c0 + HD], head[:, q, :, :],
                   rL[:, q, :].unsqueeze(2).broadcast_to([P, TPG, HD]), ALU.mult)

        def layer_norm_step():
            if beside and next(beside[0], "end") == "end":
                beside.pop(0)

        stacked = []
        for t in range(NT):
            layer_norm_step()
            tq = t - QT
            if tq == 0:
                pairs[:] = [4]
                pe.wait(bank_free[4], bank_free[5])
            if tq >= 0:
                turn_queries(*stacked.pop(0))
            steps = project(t, (t % 2) * 2)
            next(steps)
            if t > 0:
                turn_keys(*keys)
            if tq >= 0:
                turn_queries(*stacked.pop(0))
            for h in range(REP - 1):
                if tq >= 0:
                    row_max(0, h, tq)
                if h == 1:
                    keys = split_keys(t)
                    layer_norm_step()
                    assert not beside or t < QT - 1
                    if 0 <= tq + 1 < QT:
                        stacked += [stack_queries(n, tq + 1) for n in range(2)]
                next(steps, None)
            if tq >= 0:
                row_max(0, REP - 1, tq)
        turn_keys(*keys)
        for h in range(REP):
            place_max(*split_max(0, h))
        pairs[:] = [0, 2, 4]
        pe.wait(*bank_free[0:4])
        for q in (act, dve, pool):
            q.wait(queries[NT - 1], *home, dve.last())

        wo_ready = []

        def load_wo(c):
            sp.wait(*w_used, *wo_ready[-1:])
            got = in_wo.start(sp, woraw[:], wo[:, c, :])
            pool.wait(got)
            hi = pool.do(TENSOR_COPY, Wo[:, 0, c, :], woraw[:])
            pool.wait(hi)
            wo_ready.append(pool.do(TENSOR_TENSOR, Wo[:, 1, c, :], woraw[:], Wo[:, 0, c, :], ALU.subtract))

        w_used = (pe.last(),)
        pool.wait(*w_used)
        work, outputs, maxima = [], [], []
        u = 0
        for n in range(len(groups)):
            if n == len(groups) - 1:
                pairs.remove(SPARE_BANK)
                bank_free[SPARE_BANK] = pair_free[SPARE_BANK]
            for un in range(2 * REP * (QT // 2)):
                h, hf, pair = un // QT, un // (QT // 2) % 2, un % (QT // 2)
                if work:
                    split_hi(work[-1])
                    if not lo_on_vector(work[-1]):
                        split_lo(work[-1])
                work.append(scores(n, h, hf, pair, u))
                if n + 1 < len(groups):
                    row_max(n + 1, un // QT, un % QT)
                if maxima and pair == 0:
                    place_max(*maxima.pop(0))
                if n + 1 < len(groups) and un % QT == QT - 1:
                    maxima.append(split_max(n + 1, un // QT))
                if len(work) > 1 and lo_on_vector(work[-2]):
                    split_lo(work[-2])
                if work[0]["u"] == u - LAG:
                    values(work.pop(0))
                if outputs and pair == 1:
                    store_head(*outputs.pop(0))
                if stacked and pair == 3:
                    turn_queries(*stacked.pop(0))
                if n + 2 < len(groups) and pair == 1:
                    stacked.append(stack_queries(n + 2, un // 4))
                if n == len(groups) - 1 and un % QT == 0:
                    load_wo(un // QT)
                u += 1
        split_hi(work[-1])
        for w in work[-2:]:
            if lo_on_vector(w) or w is work[-1]:
                split_lo(w)
        store_head(*outputs.pop(0))
        for w in work:
            values(w)
        store_head(*outputs.pop(0))
        for i in pairs:
            bank_free[i] = bank_free[i + 1] = pair_free[i]
        return wo_ready

    def project_out(loaded, w_ready, beside):
        heads_ready = dve.last()
        turned = []
        for t in range(NT + 2):
            if t < NT:
                turned.append((t, to_columns(t, qtok[:, t, :], heads_ready, 4 + t % 4)[1]))
            if len(turned) > 2 or t >= NT:
                tt, ready = turned.pop(0)
                b, cols = tile_columns(tt)
                bk, g = tt % 4, tt // TPG
                pe.wait(ready, bank_free[bk])
                for c in range(DC):
                    pe.wait(w_ready[c])
                    done = mm3(PS[:, bk, :], xTh[:, b, c, cols], xTl[:, b, c, cols], Wo[:, 0, c, :], Wo[:, 1, c, :],
                               c == 0, c == DC - 1)
                dve.wait(done, loaded[g])
                bank_free[bk] = X_ready[g] = dve.do(TENSOR_TENSOR, X[:, tt, :], PS[:, bk, :], X[:, tt, :], ALU.add)
                if beside and next(beside[0], "end") == "end":
                    beside.pop(0)
                if tt % TPG == TPG - 1:
                    yield g

    x1_ready, h_ready, x3_ready = [None] * NG, [None] * NG, [None] * NG
    home = [None] * NG

    def to_attention(g, beside):
        sp.wait(X_ready[g])
        home[g] = out_home[g].start(sp, group_rows(x_home, g), group_of_X(g))
        beside.append(layer_norm(g, h_ready, [7]))

    beside, wqkv_in = [], []

    def load_wqkv(slot_free):
        sp.wait(slot_free)
        wqkv_in[:] = [in_wqkv[c].start(sp, wraw[:, c, :], wqkv[:, c, :]) for c in range(DC)]

    first_ffn = ffn(x1_ready, lambda g: layer_norm(g, x1_ready, [7]), lambda: (), (SPARE - NCH) % RING,
                    list(zip(first_raw, in_first)), load_wqkv, to_attention, beside)
    next(first_ffn)
    for g in range(NG // 2, NG):
        X_ready[g] = in_x[g].start(sp, group_of_X(g), group_rows(x, g))
    comb_in = in_comb.start(sp, combS[:], comb)
    rope_in = in_rope.start(sp, ropeS[:], rope)
    finish(layer_norm(0, x1_ready, [4, 5, 6, 7]))
    finish(first_ffn)

    wo_ready = attention(h_ready, home, wqkv_in, rope_in, beside)

    loop_done = [q.last() for q in (pe, act, dve, pool)]
    for q in (act, pool, sp, dve, pe):
        q.wait(*loop_done)
    loaded = [in_x[g].start(sp, group_of_X(g), group_rows(x_home, g)) for g in range(NG)]
    beside = []
    projecting = project_out(loaded, wo_ready, beside)

    def to_output(g, beside):
        sp.wait(X_ready[g])
        out_x[g].start(sp, group_rows(out, g), group_of_X(g))

    second_ffn = ffn(x3_ready, lambda g: layer_norm(g, x3_ready, [7]), lambda: (pe.last(),), 0, None,
                     lambda slot_free: None, to_output, [])
    for g in projecting:
        if g == 0:
            next(second_ffn)
        if g < 2:
            beside.append(layer_norm(g, x3_ready, [4, 5, 6, 7]))
    while beside:
        finish(beside.pop(0))
    finish(second_ffn)
    for o in out_x:
        sp.wait((o.sem, o.count))

    block = ctx.enter_context(nc.Block())

    @block.sync
    def _(e):
        sp.emit(e)

    @block.tensor
    def _(e):
        pe.emit(e)

    @block.scalar
    def _(e):
        act.emit(e)

    @block.vector
    def _(e):
        dve.emit(e)

    @block.gpsimd
    def _(e):
        pool.emit(e)


def shape_constants():
    ident = np.eye(P, dtype=np.float32)
    sel = np.zeros((P, NCH * P), np.float32)
    for e in range(E):
        for part in range(3):
            sel[part * E + e, FS + e * F:FS + (e + 1) * F if e < E - 1 else NCH * P] = 1.0
    sel[3 * E, :FS] = 1.0
    inv = (1.0 / np.float32(10000.0) ** (np.arange(0, HD, 2, dtype=np.float32) / np.float32(HD))).astype(np.float32)
    ang = np.arange(S, dtype=np.float32)[:, None] * inv[None, :]
    cos = np.cos(ang).astype(np.float32)
    sin = np.sin(ang).astype(np.float32)
    rope = np.stack([np.concatenate([cos, cos], 1), np.concatenate([-sin, sin], 1)], 1)
    rope = np.ascontiguousarray(rope.reshape(QT, P, 2, HD).transpose(1, 0, 2, 3))
    comb = np.zeros((VCOL, E), np.float32)
    comb[:E] = comb[HD + 1:HD + 1 + E] = np.eye(E)
    return ident, sel, rope, comb


def kernel(**inputs):
    from contextlib import ExitStack
    import ml_dtypes
    import concourse.bacc as bacc
    from concourse.bass_utils import run_bass_kernel_spmd

    a = {k: np.asarray(v) for k, v in inputs.items()}
    w1 = np.concatenate([a["L0_ffn_sw1"], a["L0_ffn_rw1"].transpose(1, 0, 2).reshape(D, E * F)], axis=1)
    w3 = np.concatenate([a["L0_ffn_sw3"], a["L0_ffn_rw3"].transpose(1, 0, 2).reshape(D, E * F)], axis=1)
    w2 = np.concatenate([a["L0_ffn_sw2"], a["L0_ffn_rw2"].reshape(E * F, D)], axis=0)
    pad = NCH * P - HID
    assert TAIL == pad == P // 2

    def columns(w):
        return w.reshape(DC, P, NCH, P).transpose(2, 1, 0, 3).reshape(NCH, P, D)

    w1 = np.concatenate([w1, w3[:, HID - TAIL:]], axis=1)
    w3 = np.pad(w3, ((0, 0), (0, pad)))
    w2 = np.concatenate([w2[:HID - TAIL], np.zeros((pad, D), w2.dtype), w2[HID - TAIL:]], axis=0)
    ffn_w = np.concatenate([columns(w1), columns(w3), w2.reshape(NCH, P, D)], axis=2)

    def rows(w):
        return w.reshape(DC, P, -1).transpose(1, 0, 2)

    ident, sel, rope, comb = shape_constants()
    arrays = {
        "x": a["L0_attn_x"].reshape(TOK, D),
        "ffn_w": ffn_w,
        "gate_w": rows(a["L0_ffn_gate_w"]),
        "wqkv": rows(np.concatenate([a["L0_attn_Wq"], a["L0_attn_Wk"], a["L0_attn_Wv"]], axis=0).T),
        "wo": rows(a["L0_attn_Wo"].T),
        "sel": sel.astype(ml_dtypes.bfloat16),
        "rope": rope,
        "ident": ident,
        "comb": comb,
    }
    arrays = {k: np.ascontiguousarray(v) for k, v in arrays.items()}
    nc = bacc.Bacc("TRN2", target_bir_lowering=False, num_devices=1)
    args = {k: nc.dram_tensor(k, v.shape, mybir.dt.from_np(v.dtype), kind="ExternalInput").ap()
            for k, v in arrays.items()}
    out = nc.dram_tensor("y", (TOK, D), F32, kind="ExternalOutput").ap()
    with ExitStack() as ctx:
        macaron(nc, ctx, out=out, **args)
    got = run_bass_kernel_spmd(nc, [arrays], core_ids=[0])
    return got.results[0]["y"].reshape(B, S, D)
```
